# Optimizing a Trainium2 kernel written in Bass

```python
import numpy as np
import jax
import jax.numpy as jnp

def _softmax(x, axis=-1):
    return jax.nn.softmax(x, axis=axis)

def _gelu(x):
    return jax.nn.gelu(x, approximate=True)

def _silu(x):
    return jax.nn.silu(x)

def _sigmoid(x):
    return jax.nn.sigmoid(x)

def _layernorm(x, axis=-1, eps=1e-05):
    m = jnp.mean(x, axis=axis, keepdims=True)
    v = jnp.var(x, axis=axis, keepdims=True)
    return (x - m) / jnp.sqrt(v + eps)

def _scatter_add(tgt, idx, src, axis=0):
    return tgt.at[idx].add(src)

def _segment_sum(src, seg, n):
    return jax.ops.segment_sum(src, seg, n)
kernel_name = 'mk_prb_d1_jaxref_r8_ab3586'

def setup_inputs(seed: int=0):
    np.random.seed(seed)
    _w = jnp.asarray

    def _L0_attn_setup():
        import jax, jax.numpy as jnp
        import numpy as np
        DIMS = 256
        HEADS = 16
        HEAD_DIM = DIMS // HEADS
        B, L = (4, 512)
        key = jax.random.key(seed)
        k0, k1, k2, k3 = jax.random.split(key, 4)
        scale = 1.0 / np.sqrt(DIMS)
        return {'input_seq_embs': jax.random.normal(k0, (B, L, DIMS), dtype=jnp.float32), 'Wq': jax.random.normal(k1, (DIMS, DIMS), dtype=jnp.float32) * scale, 'Wk': jax.random.normal(k2, (DIMS, DIMS), dtype=jnp.float32) * scale, 'Wv': jax.random.normal(k3, (DIMS, DIMS), dtype=jnp.float32) * scale}
    _L0_attn_in = _L0_attn_setup()

    def _L0_ffn_setup():
        import jax, jax.numpy as jnp
        import numpy as np
        HID = 256
        N_HEADS = 16
        N_KV = 16
        HEAD_DIM = HID // N_HEADS
        N_EXP = 8
        TOP_K = 2
        MOE_I = 176
        SH_I = 704
        EPS = 1e-06
        ROPE_THETA = 1000000.0

        def _rms(x, w):
            v = jnp.mean(jnp.square(x), axis=-1, keepdims=True)
            return x * jax.lax.rsqrt(v + EPS) * w

        def _rope(q, k):
            S, D = (q.shape[1], q.shape[-1])
            inv = 1.0 / ROPE_THETA ** (jnp.arange(0, D, 2, dtype=jnp.float32) / D)
            freqs = jnp.arange(S, dtype=jnp.float32)[:, None] * inv[None, :]
            emb = jnp.concatenate([freqs, freqs], axis=-1)
            cos = jnp.cos(emb)[None, :, None, :]
            sin = jnp.sin(emb)[None, :, None, :]

            def rot(t):
                t1, t2 = (t[..., :D // 2], t[..., D // 2:])
                return jnp.concatenate([-t2, t1], axis=-1)
            return (q * cos + rot(q) * sin, k * cos + rot(k) * sin)
        key = jax.random.key(seed)
        ks = jax.random.split(key, 20)
        s = 0.02
        d = {'x': jax.random.normal(ks[0], (2, 128, HID), jnp.float32), 'w_ln1': jnp.ones((HID,), jnp.float32), 'wq': jax.random.normal(ks[1], (HID, N_HEADS * HEAD_DIM), jnp.float32) * s, 'bq': jnp.zeros((N_HEADS * HEAD_DIM,), jnp.float32), 'wk': jax.random.normal(ks[2], (HID, N_KV * HEAD_DIM), jnp.float32) * s, 'bk': jnp.zeros((N_KV * HEAD_DIM,), jnp.float32), 'wv': jax.random.normal(ks[3], (HID, N_KV * HEAD_DIM), jnp.float32) * s, 'bv': jnp.zeros((N_KV * HEAD_DIM,), jnp.float32), 'wo': jax.random.normal(ks[4], (N_HEADS * HEAD_DIM, HID), jnp.float32) * s, 'w_ln2': jnp.ones((HID,), jnp.float32), 'w_router': jax.random.normal(ks[5], (HID, N_EXP), jnp.float32) * s, 'w_gate_e': jax.random.normal(ks[6], (N_EXP, HID, MOE_I), jnp.float32) * s, 'w_up_e': jax.random.normal(ks[7], (N_EXP, HID, MOE_I), jnp.float32) * s, 'w_down_e': jax.random.normal(ks[8], (N_EXP, MOE_I, HID), jnp.float32) * s, 'w_sh_gate': jax.random.normal(ks[9], (HID, SH_I), jnp.float32) * s, 'w_sh_up': jax.random.normal(ks[10], (HID, SH_I), jnp.float32) * s, 'w_sh_down': jax.random.normal(ks[11], (SH_I, HID), jnp.float32) * s, 'w_sh_eg': jax.random.normal(ks[12], (HID, 1), jnp.float32) * s}
        return d
    _L0_ffn_in = _L0_ffn_setup()
    _d = {'L0_attn_input_seq_embs': _L0_attn_in['input_seq_embs'], 'L0_attn_Wq': _L0_attn_in['Wq'], 'L0_attn_Wk': _L0_attn_in['Wk'], 'L0_attn_Wv': _L0_attn_in['Wv'], 'L0_ffn_w_ln1': _L0_ffn_in['w_ln1'], 'L0_ffn_wq': _L0_ffn_in['wq'], 'L0_ffn_bq': _L0_ffn_in['bq'], 'L0_ffn_wk': _L0_ffn_in['wk'], 'L0_ffn_bk': _L0_ffn_in['bk'], 'L0_ffn_wv': _L0_ffn_in['wv'], 'L0_ffn_bv': _L0_ffn_in['bv'], 'L0_ffn_wo': _L0_ffn_in['wo'], 'L0_ffn_w_ln2': _L0_ffn_in['w_ln2'], 'L0_ffn_w_router': _L0_ffn_in['w_router'], 'L0_ffn_w_gate_e': _L0_ffn_in['w_gate_e'], 'L0_ffn_w_up_e': _L0_ffn_in['w_up_e'], 'L0_ffn_w_down_e': _L0_ffn_in['w_down_e'], 'L0_ffn_w_sh_gate': _L0_ffn_in['w_sh_gate'], 'L0_ffn_w_sh_up': _L0_ffn_in['w_sh_up'], 'L0_ffn_w_sh_down': _L0_ffn_in['w_sh_down'], 'L0_ffn_w_sh_eg': _L0_ffn_in['w_sh_eg']}
    _x0 = _d['L0_attn_input_seq_embs']
    _d['L0_attn_input_seq_embs'] = jax.random.normal(jax.random.fold_in(jax.random.key(seed), 1), (1, 2048, 256), dtype=_x0.dtype)
    del _x0
    return _d

def reference(L0_attn_input_seq_embs, L0_attn_Wq, L0_attn_Wk, L0_attn_Wv, L0_ffn_w_ln1, L0_ffn_wq, L0_ffn_bq, L0_ffn_wk, L0_ffn_bk, L0_ffn_wv, L0_ffn_bv, L0_ffn_wo, L0_ffn_w_ln2, L0_ffn_w_router, L0_ffn_w_gate_e, L0_ffn_w_up_e, L0_ffn_w_down_e, L0_ffn_w_sh_gate, L0_ffn_w_sh_up, L0_ffn_w_sh_down, L0_ffn_w_sh_eg):

    def _L0_attn_ref(input_seq_embs, Wq, Wk, Wv):
        import jax, jax.numpy as jnp
        import numpy as np
        DIMS = 256
        HEADS = 16
        HEAD_DIM = DIMS // HEADS
        B, L = (4, 512)
        b, l, d = input_seq_embs.shape
        q = (input_seq_embs @ Wq.T).reshape(b, l, HEADS, HEAD_DIM)
        k = (input_seq_embs @ Wk.T).reshape(b, l, HEADS, HEAD_DIM)
        v = (input_seq_embs @ Wv.T).reshape(b, l, HEADS, HEAD_DIM)
        A = jnp.einsum('blhd,blgd->blhg', q, k)
        causal = jnp.tril(jnp.ones((HEADS, HEADS), dtype=bool))
        A = jnp.where(causal, A, -jnp.inf)
        A = jax.nn.softmax(A, axis=-1)
        out = jnp.einsum('blhg,blgd->blhd', A, v).reshape(b, l, d)
        return out

    def _L0_ffn_ref(x, w_ln1, wq, bq, wk, bk, wv, bv, wo, w_ln2, w_router, w_gate_e, w_up_e, w_down_e, w_sh_gate, w_sh_up, w_sh_down, w_sh_eg):
        import jax, jax.numpy as jnp
        import numpy as np
        HID = 256
        N_HEADS = 16
        N_KV = 16
        HEAD_DIM = HID // N_HEADS
        N_EXP = 8
        TOP_K = 2
        MOE_I = 176
        SH_I = 704
        EPS = 1e-06
        ROPE_THETA = 1000000.0

        def _rms(x, w):
            v = jnp.mean(jnp.square(x), axis=-1, keepdims=True)
            return x * jax.lax.rsqrt(v + EPS) * w

        def _rope(q, k):
            S, D = (q.shape[1], q.shape[-1])
            inv = 1.0 / ROPE_THETA ** (jnp.arange(0, D, 2, dtype=jnp.float32) / D)
            freqs = jnp.arange(S, dtype=jnp.float32)[:, None] * inv[None, :]
            emb = jnp.concatenate([freqs, freqs], axis=-1)
            cos = jnp.cos(emb)[None, :, None, :]
            sin = jnp.sin(emb)[None, :, None, :]

            def rot(t):
                t1, t2 = (t[..., :D // 2], t[..., D // 2:])
                return jnp.concatenate([-t2, t1], axis=-1)
            return (q * cos + rot(q) * sin, k * cos + rot(k) * sin)
        B, S, H = x.shape
        h = _rms(x, w_ln1)
        q = (h @ wq + bq).reshape(B, S, N_HEADS, HEAD_DIM)
        k = (h @ wk + bk).reshape(B, S, N_KV, HEAD_DIM)
        v = (h @ wv + bv).reshape(B, S, N_KV, HEAD_DIM)
        q, k = _rope(q, k)
        rep = N_HEADS // N_KV
        if rep > 1:
            k = jnp.repeat(k, rep, axis=2)
            v = jnp.repeat(v, rep, axis=2)
        scores = jnp.einsum('bqhd,bkhd->bhqk', q, k) * HEAD_DIM ** (-0.5)
        causal = jnp.tril(jnp.ones((S, S), bool))
        scores = jnp.where(causal[None, None], scores, jnp.finfo(scores.dtype).min)
        attn = jax.nn.softmax(scores, axis=-1)
        ctx = jnp.einsum('bhqk,bkhd->bqhd', attn, v).reshape(B, S, N_HEADS * HEAD_DIM)
        x = x + ctx @ wo
        h = _rms(x, w_ln2).reshape(B * S, H)
        logits = h @ w_router
        probs = jax.nn.softmax(logits, axis=-1)
        top_w, top_i = jax.lax.top_k(probs, TOP_K)
        combine = jnp.sum(jax.nn.one_hot(top_i, N_EXP, dtype=h.dtype) * top_w[..., None], axis=1)
        g = jnp.einsum('th,ehi->eti', h, w_gate_e)
        u = jnp.einsum('th,ehi->eti', h, w_up_e)
        y = jnp.einsum('eti,eih->eth', jax.nn.silu(g) * u, w_down_e)
        routed = jnp.einsum('eth,te->th', y, combine)
        sh = jax.nn.silu(h @ w_sh_gate) * (h @ w_sh_up) @ w_sh_down
        sh = sh * jax.nn.sigmoid(h @ w_sh_eg)
        x = x + (routed + sh).reshape(B, S, H)
        return x
    x = L0_attn_input_seq_embs
    xn = _layernorm(x, axis=-1)
    x = x + _L0_attn_ref(xn, L0_attn_Wq, L0_attn_Wk, L0_attn_Wv) + _L0_ffn_ref(xn, L0_ffn_w_ln1, L0_ffn_wq, L0_ffn_bq, L0_ffn_wk, L0_ffn_bk, L0_ffn_wv, L0_ffn_bv, L0_ffn_wo, L0_ffn_w_ln2, L0_ffn_w_router, L0_ffn_w_gate_e, L0_ffn_w_up_e, L0_ffn_w_down_e, L0_ffn_w_sh_gate, L0_ffn_w_sh_up, L0_ffn_w_sh_down, L0_ffn_w_sh_eg)
    return x

_drawn_inputs = setup_inputs


def setup_inputs(seed=0):
    import zlib

    import numpy as np

    out = dict(_drawn_inputs(seed))
    spreads = {'L0_ffn_w_ln1': (1.0, 0.6),
     'L0_ffn_bq': (0.0, 0.8),
     'L0_ffn_bk': (0.0, 0.8),
     'L0_ffn_bv': (0.0, 0.596),
     'L0_ffn_w_ln2': (1.0, 0.6)}
    factors = {'L0_ffn_wq': 8.0,
     'L0_ffn_wk': 8.0,
     'L0_ffn_wv': 8.0,
     'L0_ffn_wo': 3.853,
     'L0_ffn_w_router': 8.0,
     'L0_ffn_w_gate_e': 8.0,
     'L0_ffn_w_up_e': 8.0,
     'L0_ffn_w_down_e': 8.0,
     'L0_ffn_w_sh_gate': 7.873,
     'L0_ffn_w_sh_up': 7.794,
     'L0_ffn_w_sh_down': 7.791,
     'L0_ffn_w_sh_eg': 8.0}
    for name, (base, spread) in spreads.items():
        noise = np.random.default_rng([zlib.crc32(name.encode()), seed]).standard_normal(out[name].shape)
        drawn = base * np.exp(spread * noise) if base else spread * noise
        out[name] = jnp.asarray(drawn.astype(out[name].dtype))
    for name, factor in factors.items():
        out[name] = (out[name] * factor).astype(out[name].dtype)
    return out
```

```python
from contextlib import ExitStack

import concourse.bass as bass
from concourse import mybir

P = 128
T, D = 2048, 256
H, HD = 16, 16
NT = T // P
CH = 512
NCH = T // CH
KC = D // P
G = 4
NG = H // G
NEXP, MOE_I, SH_I = 8, 176, 704
I_ALL = NEXP * MOE_I + SH_I
NIC = -(-I_ALL // P)
NR = NEXP + 1
LN_EPS, RMS_EPS = 1e-5, 1e-6
THETA = 1000000.0
NEG = -1e30
VC = HD + 1
KROWS = 3 * HD

F32 = mybir.dt.float32
F32R = mybir.dt.float32r
BF16 = mybir.dt.bfloat16
ALU = mybir.AluOpType
ACT = mybir.ActivationFunctionType
AX = mybir.AxisListType

C_ID, C_MMAX, C_MST, C_MA = 0, 128, 256, 384
C_COS = C_MA + H * H
C_SIN = C_COS + NT * 16
C_KEY = C_SIN + NT * 32
C_ALL = C_KEY + NEXP


UNITS = [(g, c) for g in range(NG) for c in (range(NCH) if g < NG - 1 else reversed(range(NCH)))]
NU = len(UNITS)


def score_pieces():
    out = []
    for u, (g, c) in enumerate(UNITS):
        for r in range(CH // P):
            keys = P * (CH // P * c + r + 1)
            for b in range(-(-keys // CH)):
                w = min(CH, keys - b * CH)
                diagonal = (b + 1) * CH >= keys
                for pairs in ([[0, 1]] if 2 * w <= CH else [[0], [1]]):
                    for e in range(2):
                        out.append((u, r, pairs, e, b * CH, w, diagonal))
    return out


PIECES = score_pieces()
STEPS = [(u, kb) for u, (g, c) in enumerate(UNITS) for kb in range(CH // P * (c + 1))]
NS = len(STEPS)
UNIT_FIRST = [STEPS.index((u, 0)) for u in range(NU)]
UNIT_LAST = [s - 1 for s in UNIT_FIRST[1:]] + [NS - 1]
PIECE_END = [max(i for i, p in enumerate(PIECES) if p[0] == u) + 1 for u in range(NU)]
GAPS, LEAD = 3, 6


def first_key_column(s):
    u, kb = STEPS[s]
    return max(0, kb * P - UNITS[u][1] * CH)


def pieces_by_gap():
    cost = [p[5] * len(p[2]) + 100 for p in PIECES]
    share = [1 / GAPS] * GAPS
    given = [[0] * GAPS for _ in range(NS)]
    i, owed = len(PIECES), 0.0
    for s in reversed(range(NS)):
        for gap in reversed(range(GAPS)):
            given[s][gap] = i
            owed += RATE * share[gap] * 4 * (CH - first_key_column(s))
            while i and (owed > 0):
                if s > UNIT_FIRST[PIECES[i - 1][0]] - LEAD:
                    owed = min(owed, 0.0)
                    break
                i -= 1
                owed -= cost[i]
    return i, given


RATE = 1.2
AHEAD, GIVEN = pieces_by_gap()
MAX_STEP = [-1 if AHEAD >= e else next(s for s in range(NS) if GIVEN[s][-1] >= e) for e in PIECE_END]
TURNS = {}
for u in range(NU):
    TURNS.setdefault(MAX_STEP[u] + 1 if MAX_STEP[u] >= 0 else -1, []).append(("neg", u))
for u in range(NU):
    TURNS.setdefault(UNIT_LAST[u] + 1, []).append(("ctx", u))


def bank_plan():
    plan, done = {}, 0

    def give(place, upto):
        nonlocal done
        plan.setdefault(place, []).extend(("piece", i) for i in range(done, upto))
        done = max(done, upto)

    for turn in TURNS.get(-1, []):
        give((-1, 0), min(PIECE_END[turn[1]] + 2, AHEAD))
        plan[-1, 0].append(turn)
    give((-1, 0), AHEAD)
    for s in range(NS + 2):
        for gap in range(GAPS):
            give((s, gap), GIVEN[s][gap] if s < NS else done)
        plan[s, GAPS - 1] += TURNS.get(s, [])
    return plan


BANK_PLAN = bank_plan()
BANK_USES = [use for place in BANK_PLAN for use in BANK_PLAN[place]]
BANK_AT = {use: n for n, use in enumerate(BANK_USES)}


def block_program(nc, x, wproj, bqkv, wln, wo, wr, wmoe, consts, sel, out, sq, sa, sx, sn, sc):
    xv = x.rearrange("(t p) d -> p t d", p=P)
    outv = out.rearrange("(t p) d -> p t d", p=P)

    with ExitStack() as ctx:
        def sb(name, shape, dt, stack=ctx):
            return stack.enter_context(nc.sbuf_tensor(name, shape, dt))

        def ps(name, shape, dt=F32, stack=ctx):
            return stack.enter_context(nc.psum_tensor(name, shape, dt))

        def sem(name):
            return ctx.enter_context(nc.semaphore(name))

        res = sb("res", [P, NT, D], F32)
        cst = sb("cst", [P, C_ALL], F32)
        identb = sb("identb", [P, P], BF16)
        mmaxb = sb("mmaxb", [P, P], BF16)
        mstb = sb("mstb", [P, P], BF16)
        lnw = sb("lnw", [P, 2, KC], F32)
        bias = sb("bias", [P, 3 * D], F32)
        zb = sb("zb", [P, CH], BF16)
        ident = cst[:, C_ID:C_ID + P]
        mask_a = cst[:, C_MA:C_MA + H * H].rearrange("p (h g) -> p h g", h=H)

        s2 = ExitStack()
        qs = [sb("qs0", [P, 2, 2, T], F32R, s2)]
        ks = [sb("ks0", [P, 2, T], F32R, s2)]
        v = sb("v", [P, NT, H, VC], F32, s2)
        s12 = s2.enter_context(ExitStack())
        qs.append(sb("qs1", [P, 2, 2, T], F32R, s12))
        ks.append(sb("ks1", [P, 2, T], F32R, s12))
        pt = sb("pt", [P, 2, 2, 2, CH], F32, s12)
        ain = sb("ain", [P, 2, 3 * D], F32, s12)
        qkp = [sb(f"qkp{b}", [P, 4, 4 * (b + 1), HD], F32, s12) for b in range(4)]
        avp = [sb(f"avp{b}", [P, 4, 4 * (b + 1), HD], F32, s12) for b in range(4)]
        alog = sb("alog", [P, H, H], F32, s12)
        amask = sb("amask", [P, H, H], F32, s12)
        ashift = sb("ashift", [P, H, H], F32, s12)
        aexp = sb("aexp", [P, H, H], F32, s12)
        amx = sb("amx", [P, H], F32, s12)
        asum = sb("asum", [P, H], F32, s12)
        arec = sb("arec", [P, H], F32, s12)
        aout = sb("aout", [P, H, HD], F32, s12)
        ascl = sb("ascl", [P, H, HD], F32, s12)
        mxp = sb("mxp", [P, 2, CH // P, 2, 2, NCH], F32, s12)
        nmx = sb("nmx", [P, CH // P, 2, 2], F32, s12)
        nmt = sb("nmt", [P, 2, CH // P, 8], F32R, s12)
        nmr = sb("nmr", [8, 2, CH], F32, s12)
        osb = sb("osb", [P, CH], F32, s12)
        orec = sb("orec", [P, CH // P, G], F32, s12)
        ctxs = sb("ctxs", [P, 2, CH // P, G * HD], F32, s12)
        s12.close()
        s1 = ExitStack()
        xn = sb("xn", [P, NT, D], F32, s1)
        wraw = sb("wraw", [P, KC, 6 * D], F32, s1)
        wh = sb("wh", [P, KC, 6 * D], F32R, s1)
        wl = sb("wl", [P, KC, 6 * D], F32R, s1)
        xnp = sb("xnp", [P, 2, D], F32, s1)
        xh = sb("xh", [P, 2, KC, P], F32R, s1)
        xl = sb("xl", [P, 2, KC, P], F32R, s1)
        qksb = sb("qksb", [P, 2, 2 * D], F32, s1)
        vst = sb("vst", [P, 2, D], F32, s1)
        asb = sb("asb", [P, 2, 3 * D], F32, s1)
        rt1 = sb("rt1", [P, 2, 2 * D], F32, s1)
        rt2 = sb("rt2", [P, 2, 2 * D], F32, s1)
        qkr = sb("qkr", [P, 2, 2 * D], F32, s1)
        sth = sb("sth", [P, 2, 4, P], F32R, s1)
        stl = sb("stl", [P, 2, 4, P], F32R, s1)
        bst = sb("bst", [P, NT, 6], F32, s1)
        mv = sb("mv", [P, NT, 2], F32, s1)
        tmpr = sb("tmpr", [P, NT], F32, s1)
        rstd = sb("rstd", [P, NT], F32, s1)
        rms1 = sb("rms1", [P, NT], F32, s1)
        half = sb("half", [P, 4], F32, s1)
        s1.close()
        s2.close()
        s3 = ExitStack()
        mh, ml = [], []
        for ic in range(NIC):
            mh.append(sb(f"mh{ic}", [P, 6, P], F32R, s3))
            ml.append(sb(f"ml{ic}", [P, 6, P], F32R, s3))
        mraw = sb("mraw", [P, 2, 6, P], F32, s3)
        woraw = sb("woraw", [P, KC, D], F32, s3)
        woh = sb("woh", [P, KC, D], F32R, s3)
        wol = sb("wol", [P, KC, D], F32R, s3)
        wrraw = sb("wrraw", [P, KC, NR], F32, s3)
        wrh = sb("wrh", [P, KC, NR], F32R, s3)
        wrl = sb("wrl", [P, KC, NR], F32R, s3)
        selb = sb("selb", [P, NIC * P], BF16, s3)
        ctxin = sb("ctxin", [P, 4, D], F32, s3)
        xin = sb("xin", [P, 4, D], F32, s3)
        cth = sb("cth", [P, KC, CH], F32R, s3)
        ctl = sb("ctl", [P, KC, CH], F32R, s3)
        x1 = sb("x1", [P, 4, D], F32, s3)
        sqj = sb("sqj", [P, D], F32, s3)
        hth = sb("hth", [P, 2, KC, CH], F32R, s3)
        htl = sb("htl", [P, 2, KC, CH], F32R, s3)
        lg = sb("lg", [NR, CH], F32, s3)
        combt = sb("combt", [P, 2, CH], BF16, s3)
        cbt = sb("cbt", [P, 4, 32], BF16, s3)
        th = sb("th", [P, 2, CH], F32, s3)
        act_f = sb("act_f", [P, 2, CH], F32, s3)
        act_h = sb("act_h", [P, 2, CH], F32R, s3)
        act_l = sb("act_l", [P, 2, CH], F32R, s3)
        msq = sb("msq", [P, 4], F32, s3)
        msq1 = sb("msq1", [P, 4], F32, s3)
        rms2 = sb("rms2", [P, 4], F32, s3)
        half3 = sb("half3", [P, 4], F32, s3)
        lt = sb("lt", [P, 4, NR], F32, s3)
        rt = {n: sb(f"rt_{n}", [P, 4, NEXP], F32, s3) for n in ("d", "e", "p", "is", "key", "oh1", "oh2", "p2", "oh")}
        rs4 = {n: sb(f"rs_{n}", [P, 4], F32, s3) for n in ("mx", "sum", "rec", "m1", "k1", "m2", "k2")}
        sg = sb("sg", [P, 4], F32, s3)
        cw = sb("cw", [P, 4, NR], F32, s3)
        cwr = sb("cwr", [P, 2, 4, NR], F32, s3)
        s3.close()

        p1 = ExitStack()
        tp = ps("tp", [P, CH], F32, p1)
        qt = ps("qt", [P, 4, P], F32, p1)
        pqk = [ps(f"pqk{i}", [P, CH], F32, p1) for i in range(2)]
        pva = [ps(f"pva{i}", [P, CH], F32, p1) for i in range(2)]
        pka = [ps(f"pka{i}", [P, CH], F32, p1) for i in range(2)]
        p1.close()
        p2 = ExitStack()
        mx = [ps(f"mx{i}", [P, CH], F32, p2) for i in range(3)]
        st = [ps(f"st{i}", [P, 2, CH], F32, p2) for i in range(2)]
        o = ps("o", [P, CH], F32, p2)
        p2.close()

        p3 = ExitStack()
        pg = [ps(f"pg{i}", [P, CH], F32, p3) for i in range(2)]
        pu = [ps(f"pu{i}", [P, CH], F32, p3) for i in range(2)]
        pc = ps("pc", [P, CH], F32, p3)
        py = [ps(f"py{i}", [P, CH], F32, p3) for i in range(2)]
        side = ps("side", [P, CH], F32, p3)
        p3.close()

        x_in = sem("x_in")
        w_in = sem("w_in")
        c_in = sem("c_in")
        b_in = sem("b_in")
        cst_bf = sem("cst_bf")
        half_set = sem("half_set")
        stats = sem("stats")
        rs_ln = sem("rs_ln")
        rs_rms = sem("rs_rms")
        rs_step = sem("rs_step")
        w_scaled = sem("w_scaled")
        w_hi = sem("w_hi")
        w_lo = sem("w_lo")
        xn_done = sem("xn_done")
        tp_ready = sem("tp_ready")
        x_hi = sem("x_hi")
        x_lo = sem("x_lo")
        mm_qk = sem("mm_qk")
        mm_va = sem("mm_va")
        mm_ka = sem("mm_ka")
        e_qk = sem("e_qk")
        e_v = sem("e_v")
        e_a = sem("e_a")
        biased = sem("biased")
        v_done = sem("v_done")
        rot_sin = sem("rot_sin")
        rot_cos = sem("rot_cos")
        roped = sem("roped")
        qt_ready = sem("qt_ready")
        q_hi = sem("q_hi")
        q_lo = sem("q_lo")
        sq_out = [sem(f"sq_out{i}") for i in range(2)]
        sa_out = [sem(f"sa_out{i}") for i in range(2)]
        sx_out = sem("sx_out")
        v_ones = sem("v_ones")
        q_zero = [sem(f"q_zero{i}") for i in range(2)]
        k_ones = [sem(f"k_ones{i}") for i in range(2)]
        stk_in = [sem(f"stk_in{i}") for i in range(2)]
        mx_ready = sem("mx_ready")
        mx_read = sem("mx_read")
        nm_step = sem("nm_step")
        nm_ready = sem("nm_ready")
        nt_ready = sem("nt_ready")
        bn = sem("bn")
        nr_ready = sem("nr_ready")
        nr_out = [sem(f"nr_out{i}") for i in range(2)]
        nr_in = [sem(f"nr_in{i}") for i in range(4)]
        st_ready = sem("st_ready")
        exped = sem("exped")
        av_done = sem("av_done")
        o_zero = sem("o_zero")
        o_read = sem("o_read")
        ot_ready = sem("ot_ready")
        o_rec = sem("o_rec")
        ctx_ready = sem("ctx_ready")
        ctx_out = [sem(f"ctx_out{i}") for i in range(2)]
        a_in = [sem(f"a_in{i}") for i in range(2)]
        a_prod = sem("a_prod")
        a_log = sem("a_log")
        a_masked = sem("a_masked")
        a_max = sem("a_max")
        a_shift = sem("a_shift")
        a_exp = sem("a_exp")
        a_sum = sem("a_sum")
        a_rec = sem("a_rec")
        a_tree = sem("a_tree")
        a_done = sem("a_done")
        att_end = sem("att_end")
        ws_in = sem("ws_in")
        sel_in = sem("sel_in")
        c3_set = sem("c3_set")
        half3_set = sem("half3_set")
        sel_zero = sem("sel_zero")
        m_in = [sem(f"m_in{i}") for i in range(2)]
        m_hi = sem("m_hi")
        m_lo = sem("m_lo")
        ws_hi = sem("ws_hi")
        ws_lo = sem("ws_lo")
        cx_in = sem("cx_in")
        xr_in = sem("xr_in")
        sd_ready = sem("sd_ready")
        sd_hi = sem("sd_hi")
        sd_read = sem("sd_read")
        x1_ready = sem("x1_ready")
        sq_done = sem("sq_done")
        ms_step = sem("ms_step")
        r2_ready = sem("r2_ready")
        res_x1 = sem("res_x1")
        hn_ready = sem("hn_ready")
        lt_done = sem("lt_done")
        rt_step = sem("rt_step")
        rt_exp = sem("rt_exp")
        cb_ready = sem("cb_ready")
        comb_ready = sem("comb_ready")
        g_ready = sem("g_ready")
        u_ready = sem("u_ready")
        c_ready = sem("c_ready")
        th_ready = sem("th_ready")
        act_step = sem("act_step")
        f_ready = sem("f_ready")
        ah_ready = sem("ah_ready")
        al_ready = sem("al_ready")
        y_used = sem("y_used")
        y_read = sem("y_read")
        out_ready = sem("out_ready")
        fin = sem("fin")

        def tiles(eng, step):
            for m in range(2):
                step(m, 0)
                step(m, 1)
            with eng.Fori(2, NT // 2 - 1) as m:
                step(m, 0)
                step(m, 1)
            step(NT // 2 - 1, 0)
            step(NT // 2 - 1, 1)

        def at_least(tile, n):
            return not isinstance(tile, int) or tile >= n

        def at_most(tile, n):
            return not isinstance(tile, int) or tile <= n

        MAXIMA, EXPS, SUMS = 4, 5, 6
        A_STEPS = {0: 0, 1: 1, 2: 2, 3: 3, MAXIMA: 5, EXPS: 8, SUMS: 9}
        a_steps = {}
        for t in range(NT):
            base = t * (NS // NT)
            for kind, step in A_STEPS.items():
                a_steps.setdefault(base + step, []).append((kind, t))

        OUTPUT = {1: "y_copy", 2: "out_a", 3: "out_b"}
        PREPARE = {4: "turn_ctx0", 5: "turn_ctx1", 6: "proj_a", 7: "proj_b", 9: "normalise", 10: "turn_h0",
                   11: "turn_h1", 12: "logits", 13: "turn_logits", 14: "softmax", 15: "top2", 16: "turn_comb"}
        PREP_ORDER = [PREPARE[k] for k in sorted(PREPARE)]
        BANKED = ("turn_ctx0", "turn_ctx1", "proj_a", "proj_b", "turn_h0", "turn_h1", "logits", "turn_logits",
                  "turn_comb", "out_a", "out_b")

        def side_plan():
            plan = [(-1, w, 0) for w in PREP_ORDER]
            for c in range(NCH + 1):
                for ic in range(NIC):
                    if c >= 1 and ic in OUTPUT:
                        plan.append((c * NIC + ic, OUTPUT[ic], c - 1))
                    if c + 1 < NCH and ic in PREPARE:
                        plan.append((c * NIC + ic, PREPARE[ic], c + 1))
            return plan

        SIDE = side_plan()
        side_use = {(w, c): n for n, (w, c) in enumerate((w, c) for _, w, c in SIDE if w in BANKED)}
        M3 = NCH * NIC
        MS_AFTER = 3

        def run_side(step, do):
            for at, w, c in SIDE:
                if at == step:
                    do(w, c)

        block = ctx.enter_context(nc.Block())

        @block.sync
        def _(sp):
            sp.dma_start(cst[:, :], consts).then_inc(c_in, 16)
            for c in range(NCH):
                sp.dma_start(res[:, 4 * c:4 * c + 4, :], xv[:, 4 * c:4 * c + 4, :]).then_inc(x_in, 16)
                if c == 0:
                    sp.dma_start(lnw[:, :, :], wln).then_inc(b_in, 16)
                    sp.dma_start(bias[:, :], bqkv.partition_broadcast(P)).then_inc(b_in, 16)
                    sp.dma_start(wraw[:, :, :], wproj.rearrange("(k p) n -> p k n", p=P)).then_inc(w_in, 16)
                sp.wait_ge(x_in, 16 * (c + 1))

            def qk_out(m, par):
                sp.wait_ge(q_lo, 2 * m + par + 1)
                for piece, src in ((0, sth), (1, stl)):
                    sp.dma_start(sq[piece].rearrange("(c p) n -> p c n", p=P)[:, :, bass.ds((2 * m + par) * P, P)],
                                 src[:, par, :, :].bitcast(F32)).then_inc(sq_out[par], 16)

            def step(m, par):
                t = 2 * m + par
                if at_least(t, 1):
                    if par:
                        qk_out(m, 0)
                    else:
                        qk_out(m - 1, 1)
                sp.wait_ge(e_a, t + 1)
                sp.dma_start(sa[bass.ds(t, 1), :, :].rearrange("a p n -> p (a n)"), asb[:, par, :]).then_inc(sa_out[par], 16)

            tiles(sp, step)
            qk_out(NT // 2 - 1, 1)
            sp.wait_ge(xn_done, NT)
            sp.dma_start(sx, xn[:, :, :]).then_inc(sx_out, 16)
            for par in range(2):
                sp.wait_ge(sq_out[par], 32 * (NT // 2))
                sp.wait_ge(sa_out[par], 16 * (NT // 2))

            def load_stack(g):
                for dst, base, order in ((qs, 0, (0, 0, 1)), (ks, D, (0, 1, 0))):
                    for b, piece in enumerate(order):
                        src = sq[piece][base + 64 * g:base + 64 * g + 64, :].rearrange("(s e d) n -> e d s n", s=2, e=2)
                        for e in range(2):
                            rows = slice(KROWS * e + HD * b, KROWS * e + HD * b + HD)
                            into = qs[g % 2][rows, :, e, :] if dst is qs else ks[g % 2][rows, :, :]
                            sp.dma_start(into.bitcast(F32), src[e]).then_inc(stk_in[g % 2], 16)

            sp.wait_ge(k_ones[0], 1)
            load_stack(0)
            sp.wait_ge(k_ones[1], 1)
            load_stack(1)

            def load_a(t):
                if t >= 2:
                    sp.wait_ge(a_done, t - 1)
                sp.dma_start(ain[:, t % 2, :], sa[t]).then_inc(a_in[t % 2], 16)

            sp.wait_ge(sx_out, 16)
            sp.wait_ge(v_done, NT)
            sp.wait_ge(mm_ka, NT)
            load_a(0)
            load_a(1)
            next_a = 2

            for s in range(-1, NS + 3):
                for kind, u in TURNS.get(s - 1, []) if s > -1 else []:
                    g, c = UNITS[u]
                    if kind == "neg":
                        sp.wait_ge(nr_ready, u + 1)
                        sp.dma_start(sn[u], nmr[:, u % 2, :]).then_inc(nr_out[u % 2], 16)
                        sp.wait_ge(nr_out[u % 2], 16 * (u // 2 + 1))
                        for e in range(2):
                            sp.dma_start(qs[g % 2][2 * KROWS:2 * KROWS + 2, :, e, c * CH:(c + 1) * CH].bitcast(F32),
                                         sn[u, 4 * e:4 * e + 4, :].rearrange("(a b) n -> a b n", a=2)).then_inc(nr_in[u % 4], 16)
                for u in range(NU):
                    if s == UNIT_LAST[u] + 3:
                        g, c = UNITS[u]
                        sp.wait_ge(ctx_ready, u + 1)
                        sp.dma_start(sc[:, 4 * c:4 * c + 4, 64 * g:64 * g + 64], ctxs[:, u % 2, :, :]).then_inc(ctx_out[u % 2], 16)
                        if u % NCH == NCH - 1 and g + 2 < NG:
                            sp.wait_ge(av_done, UNIT_LAST[u] + 1)
                            load_stack(g + 2)
                if next_a < NT and s == (next_a - 1) * (NS // NT):
                    load_a(next_a)
                    next_a += 1

            sp.wait_ge(att_end, 4)
            for i in range(2):
                sp.wait_ge(ctx_out[i], 16 * NU // 2)
            for i in range(4):
                sp.wait_ge(nr_in[i], 32 * NU // 4)
            sp.dma_start(woraw[:, :, :], wo.rearrange("(k p) n -> p k n", p=P)).then_inc(ws_in, 16)
            sp.dma_start(wrraw[:, :, :], wr.rearrange("(k p) n -> p k n", p=P)).then_inc(ws_in, 16)

            def load_chunk(c):
                if c >= 1:
                    sp.wait_ge(sd_read, side_use["turn_h1", c - 1] + 1)
                sp.dma_start(ctxin[:, :, :], sc[:, 4 * c:4 * c + 4, :]).then_inc(cx_in, 16)
                sp.dma_start(xin[:, :, :], sx[:, 4 * c:4 * c + 4, :]).then_inc(xr_in, 16)

            load_chunk(0)
            for ic in range(NIC):
                if ic >= 2:
                    sp.wait_ge(m_lo, ic - 1)
                if ic == 6:
                    load_chunk(1)
                sp.dma_start(mraw[:, ic % 2, :, :], wmoe[ic].rearrange("p (a n) -> p a n", a=6)).then_inc(m_in[ic % 2], 16)
            for c in range(1, NCH + 1):
                if 2 <= c < NCH:
                    load_chunk(c)
                for n in range(2):
                    sp.wait_ge(out_ready, 2 * (c - 1) + n + 1)
                    t2 = slice(4 * (c - 1) + 2 * n, 4 * (c - 1) + 2 * n + 2)
                    sp.dma_start(outv[:, t2, :], res[:, t2, :]).then_inc(fin, 16)
            sp.wait_ge(fin, 16 * 2 * NCH)

        @block.gpsimd
        def _(pool):
            pool.memset(half[:, :], -0.5).then_inc(half_set, 1)
            pool.memset(v[:, :, :, HD:VC], 1.0).then_inc(v_ones, 1)
            pool.memset(qs[0][:, :, :, :].bitcast(F32), 0.0).then_inc(q_zero[0], 1)
            pool.wait_ge(half_set, 1)
            pool.wait_ge(v_ones, 1)
            pool.wait_ge(q_zero[0], 1)
            pool.memset(ks[0][96:128, :, :].bitcast(F32), 1.0).then_inc(k_ones[0], 1)
            pool.wait_ge(k_ones[0], 1)
            for c in range(NCH):
                t4 = slice(4 * c, 4 * c + 4)
                pool.wait_ge(stats, c + 1)
                pool.tensor_scalar(tmpr[:, t4], mv[:, t4, 1], LN_EPS, None, ALU.add).then_inc(rs_step, 1)
                pool.wait_ge(rs_step, 4 * c + 1)
                pool.tensor_tensor(rstd[:, t4], tmpr[:, t4], half[:, :], ALU.pow).then_inc(rs_ln, 4)
                pool.wait_ge(rs_ln, 4 * c + 4)
                pool.tensor_tensor(tmpr[:, t4], rstd[:, t4], rstd[:, t4], ALU.mult).then_inc(rs_step, 1)
                pool.wait_ge(rs_step, 4 * c + 2)
                pool.tensor_tensor(tmpr[:, t4], tmpr[:, t4], mv[:, t4, 1], ALU.mult).then_inc(rs_step, 1)
                pool.wait_ge(rs_step, 4 * c + 3)
                pool.tensor_scalar(tmpr[:, t4], tmpr[:, t4], RMS_EPS, None, ALU.add).then_inc(rs_step, 1)
                pool.wait_ge(rs_step, 4 * c + 4)
                pool.tensor_tensor(rms1[:, t4], tmpr[:, t4], half[:, :], ALU.pow).then_inc(rs_rms, 4)

            pool.wait_ge(b_in, 32)
            pool.wait_ge(c_in, 16)

            def step(m, par):
                t = 2 * m + par
                pool.wait_ge(e_qk, t + 1)
                pool.tensor_tensor(qksb[:, par, :], qksb[:, par, :], bias[:, 0:2 * D], ALU.add).then_inc(biased, 1)
                pool.wait_ge(e_v, t + 1)
                pool.tensor_tensor(v[:, bass.ds(t, 1), :, 0:HD].rearrange("p a h d -> p (a h) d"),
                                   vst[:, par, :].rearrange("p (h d) -> p h d", h=H),
                                   bias[:, 2 * D:3 * D].rearrange("p (h d) -> p h d", h=H), ALU.add).then_inc(v_done, 1)
                pool.wait_ge(biased, t + 1)
                if at_least(t, 2):
                    pool.wait_ge(roped, t - 1)
                src = qksb[:, par, :].rearrange("p (q h f e) -> p q h f e", q=2, h=H, f=2)
                dst = rt2[:, par, :].rearrange("p (q h f e) -> p q h f e", q=2, h=H, f=2)
                sn_t = cst[:, bass.ds(C_SIN + t * 32, 32)].rearrange("p (q f e) -> p q f e", q=2, f=2)
                for f in range(2):
                    last = pool.tensor_tensor(dst[:, :, :, f, :], src[:, :, :, 1 - f, :],
                                              sn_t[:, :, f, :].unsqueeze(2).broadcast_to([P, 2, H, 8]), ALU.mult)
                last.then_inc(rot_sin, 1)

            tiles(pool, step)
            pool.wait_ge(roped, NT)
            pool.wait_ge(q_lo, NT)
            pool.wait_ge(mm_ka, NT)
            pool.wait_ge(sx_out, 16)
            for i in range(2):
                pool.wait_ge(sa_out[i], 16 * (NT // 2))
                pool.wait_ge(sq_out[i], 32 * (NT // 2))

            pool.memset(qs[1][:, :, :, :].bitcast(F32), 0.0).then_inc(q_zero[1], 1)
            pool.wait_ge(q_zero[1], 1)
            pool.memset(ks[1][96:128, :, :].bitcast(F32), 1.0).then_inc(k_ones[1], 1)
            pool.wait_ge(k_ones[1], 1)

            def products(t, m, par):
                pool.wait_ge(a_in[par], 16 * (m + 1))
                if at_least(t, 1):
                    pool.wait_ge(a_log, t)
                for b in range(4):
                    n = 4 * (b + 1)
                    q = ain[:, par, 4 * b * HD:4 * (b + 1) * HD].rearrange("p (h d) -> p h d", d=HD)
                    k = ain[:, par, D:D + n * HD].rearrange("p (g d) -> p g d", d=HD)
                    last = pool.tensor_tensor(qkp[b][:, :, :, :], q.unsqueeze(2).broadcast_to([P, 4, n, HD]),
                                              k.unsqueeze(1).broadcast_to([P, 4, n, HD]), ALU.mult)
                last.then_inc(a_prod, 1)

            TREE_ALL = 4 + 13 + 1

            def token_tile(m, par, last_tile=False):
                t = 2 * m + par
                pool.wait_ge(a_log, t + 1)
                pool.tensor_tensor(amask[:, :, :], alog[:, :, :], mask_a, ALU.add).then_inc(a_masked, 1)
                if not last_tile:
                    products(t + 1, m + par, 1 - par)
                pool.wait_ge(a_max, t + 1)
                pool.tensor_tensor(ashift[:, :, :], amask[:, :, :], amx[:, :].unsqueeze(2).broadcast_to([P, H, H]),
                                   ALU.subtract).then_inc(a_shift, 1)
                pool.wait_ge(a_exp, t + 1)
                if at_least(t, 1):
                    pool.wait_ge(a_done, t)
                for b in range(4):
                    n = 4 * (b + 1)
                    vv = ain[:, par, 2 * D:2 * D + n * HD].rearrange("p (g d) -> p g d", d=HD)
                    pool.tensor_tensor(avp[b][:, :, :, :], aexp[:, 4 * b:4 * b + 4, 0:n].unsqueeze(3).broadcast_to([P, 4, n, HD]),
                                       vv.unsqueeze(1).broadcast_to([P, 4, n, HD]), ALU.mult).then_inc(a_tree, 1)
                left = {b: 4 * (b + 1) for b in range(4)}
                pending = {b: b + 1 for b in range(4)}
                issued = 4
                while left:
                    for b in sorted(left):
                        n = left[b]
                        pool.wait_ge(a_tree, t * TREE_ALL + pending[b])
                        if n == 2:
                            dst, lo, hi = aout[:, 4 * b:4 * b + 4, :], avp[b][:, :, 0, :], avp[b][:, :, 1, :]
                        elif n == 3:
                            dst, lo, hi = avp[b][:, :, 0, :], avp[b][:, :, 0, :], avp[b][:, :, 2, :]
                        else:
                            dst, lo, hi = (avp[b][:, :, 0:n // 2, :].rearrange("p h g d -> p h (g d)"),
                                           avp[b][:, :, 0:n // 2, :].rearrange("p h g d -> p h (g d)"),
                                           avp[b][:, :, n // 2:n, :].rearrange("p h g d -> p h (g d)"))
                        pool.tensor_tensor(dst, lo, hi, ALU.add).then_inc(a_tree, 1)
                        issued += 1
                        pending[b] = issued
                        if n == 2:
                            del left[b]
                        else:
                            left[b] = 2 if n == 3 else n // 2
                assert issued + 1 == TREE_ALL
                pool.wait_ge(a_rec, t + 1)
                pool.wait_ge(a_tree, t * TREE_ALL + issued)
                pool.tensor_tensor(ascl[:, :, :], aout[:, :, :], arec[:, :].unsqueeze(2).broadcast_to([P, H, HD]),
                                   ALU.mult).then_inc(a_tree, 1)
                pool.wait_ge(a_tree, t * TREE_ALL + issued + 1)
                rt = res[:, bass.ds(t, 1), :].rearrange("p a d -> p (a d)")
                pool.tensor_tensor(rt, rt, ascl[:, :, :].rearrange("p h d -> p (h d)"), ALU.add).then_inc(a_done, 1)

            products(0, 0, 0)
            token_tile(0, 0)
            token_tile(0, 1)
            with pool.Fori(1, NT // 2 - 1) as m:
                token_tile(m, 0)
                token_tile(m, 1)
            token_tile(NT // 2 - 1, 0)
            token_tile(NT // 2 - 1, 1, last_tile=True)


            pool.wait_ge(a_done, NT)
            pool.sem_inc(att_end, 1)
            pool.wait_ge(att_end, 4)
            pool.memset(selb[:, :], 0.0).then_inc(sel_zero, 1)
            pool.memset(half3[:, :], -0.5).then_inc(half3_set, 1)
            pool.wait_ge(sel_zero, 1)
            pool.dma_start(selb[0:3 * NR, :], sel).then_inc(sel_in, 16)
            pool.wait_ge(ws_in, 32)
            pool.wait_ge(ws_hi, 2)
            pool.tensor_tensor(wol[:, :, :], woraw[:, :, :], woh[:, :, :].bitcast(F32), ALU.subtract).then_inc(ws_lo, 1)
            pool.tensor_tensor(wrl[:, :, :], wrraw[:, :, :], wrh[:, :, :].bitcast(F32), ALU.subtract).then_inc(ws_lo, 1)
            pool.wait_ge(half3_set, 1)

            def mean_squares(c):
                pool.wait_ge(sq_done, c + 1)
                pool.tensor_scalar(msq1[:, :], msq[:, :], 1.0 / D, RMS_EPS, ALU.mult, ALU.add).then_inc(ms_step, 1)
                pool.wait_ge(ms_step, c + 1)
                pool.tensor_tensor(rms2[:, :], msq1[:, :], half3[:, :], ALU.pow).then_inc(r2_ready, 1)
                rt4 = res[:, 4 * c:4 * c + 4, :]
                pool.tensor_tensor(rt4, rt4, x1[:, :, :], ALU.add).then_inc(res_x1, 1)

            for ic in range(NIC):
                pool.wait_ge(m_hi, ic + 1)
                pool.tensor_tensor(ml[ic][:, :, :], mraw[:, ic % 2, :, :], mh[ic][:, :, :].bitcast(F32),
                                   ALU.subtract).then_inc(m_lo, 1)
                if ic == MS_AFTER:
                    mean_squares(0)
            for c in range(1, NCH):
                mean_squares(c)

        @block.scalar
        def _(act):
            for n in range(3):
                if n < 2:
                    act.wait_ge(w_scaled, n + 1)
                act.activation(wh[:, :, n * CH:(n + 1) * CH], wraw[:, :, n * CH:(n + 1) * CH], ACT.Copy).then_inc(w_hi, 1)

            def hi_of_x(t, par):
                act.wait_ge(tp_ready, t + 1)
                if at_least(t, 2):
                    act.wait_ge(mm_ka, t - 1)
                act.activation(xh[:, par, :, :], tp[:, 0:KC * P].rearrange("p (k n) -> p k n", k=KC), ACT.Copy).then_inc(x_hi, 1)

            def hi_of_q(m, par):
                t = 2 * m + par
                act.wait_ge(qt_ready, t + 1)
                if at_least(m, 1):
                    act.wait_ge(sq_out[par], 32 * m)
                act.activation(sth[:, par, :, :], qt[:, :, :], ACT.Copy).then_inc(q_hi, 1)

            hi_of_x(0, 0)
            act.wait_ge(rs_rms, 4)

            def step(m, par):
                t = 2 * m + par
                if at_most(t, NT - 2):
                    hi_of_x(t + 1, 1 - par)
                scale = rms1[:, bass.ds(t, 1)]
                act.wait_ge(rs_rms, t + 1)
                act.wait_ge(mm_qk, t + 1)
                if at_least(t, 2):
                    act.wait_ge(roped, t - 1)
                act.activation(qksb[:, par, :], pqk[par][:, :], ACT.Copy, scale=scale).then_inc(e_qk, 1)
                act.wait_ge(mm_va, t + 1)
                if at_least(t, 2):
                    act.wait_ge(v_done, t - 1)
                if at_least(m, 1):
                    act.wait_ge(sa_out[par], 16 * m)
                act.activation(asb[:, par, 0:D], pva[par][:, D:2 * D], ACT.Copy)
                act.activation(vst[:, par, :], pva[par][:, 0:D], ACT.Copy, scale=scale).then_inc(e_v, 1)
                act.wait_ge(mm_ka, t + 1)
                act.activation(asb[:, par, D:3 * D], pka[par][:, :], ACT.Copy).then_inc(e_a, 1)
                if at_least(t, 1):
                    if par:
                        hi_of_q(m, 0)
                    else:
                        hi_of_q(m - 1, 1)

            tiles(act, step)
            hi_of_q(NT // 2 - 1, 1)
            act.wait_ge(q_lo, NT)
            act.wait_ge(v_done, NT)
            act.wait_ge(sx_out, 16)
            for i in range(2):
                act.wait_ge(sa_out[i], 16 * (NT // 2))
                act.wait_ge(sq_out[i], 32 * (NT // 2))

            def exp_pair(s, pr):
                off = first_key_column(s)
                act.wait_ge(st_ready, 2 * s + pr + 1)
                if s >= 2:
                    act.wait_ge(av_done, s - 1)
                act.activation(pt[:, s % 2, pr, :, off:CH], st[pr][:, :, off:CH], ACT.Exp).then_inc(exped, 1)

            def neg_rows(u):
                act.wait_ge(nt_ready, u + 1)
                if u >= 2:
                    act.wait_ge(nr_out[u % 2], 16 * (u // 2))
                act.activation(nmr[:, u % 2, :], mx[BANK_AT["neg", u] % 3][0:8, :], ACT.Copy).then_inc(nr_ready, 1)

            for s in range(-1, NS + 3):
                if 0 <= s < NS:
                    exp_pair(s, 0)
                if s - 1 in UNIT_LAST:
                    u = UNIT_LAST.index(s - 1)
                    act.wait_ge(av_done, s)
                    if u >= 1:
                        act.wait_ge(ot_ready, u)
                    act.activation(osb[:, :], o[:, :], ACT.Copy).then_inc(o_read, 1)
                if 0 <= s < NS:
                    exp_pair(s, 1)
                for kind, u in TURNS.get(s, []):
                    if kind == "neg":
                        neg_rows(u)
                for kind, t in a_steps.get(s, []):
                    if kind == EXPS:
                        act.wait_ge(a_shift, t + 1)
                        if t >= 1:
                            act.wait_ge(a_tree, 18 * (t - 1) + 4)
                        act.activation(aexp[:, :, :], ashift[:, :, :], ACT.Exp).then_inc(a_exp, 1)


            act.wait_ge(o_read, NU)
            act.sem_inc(att_end, 1)
            act.wait_ge(att_end, 4)
            act.wait_ge(ws_in, 32)
            act.activation(woh[:, :, :], woraw[:, :, :], ACT.Copy).then_inc(ws_hi, 1)
            act.activation(wrh[:, :, :], wrraw[:, :, :], ACT.Copy).then_inc(ws_hi, 1)

            def split_weights(ic):
                act.wait_ge(m_in[ic % 2], 16 * (ic // 2 + 1))
                act.activation(mh[ic][:, :, :], mraw[:, ic % 2, :, :], ACT.Copy).then_inc(m_hi, 1)

            def side_act(w, c):
                if w in BANKED:
                    ready = side_use[w, c] + 1
                if w in ("turn_ctx0", "turn_ctx1"):
                    act.wait_ge(sd_ready, ready)
                    act.activation(cth[:, int(w[-1]), :], side[:, :], ACT.Copy).then_inc(sd_hi, 1)
                elif w in ("turn_h0", "turn_h1"):
                    k = int(w[-1])
                    act.wait_ge(sd_ready, ready)
                    act.activation(hth[:, c % 2, k, :], side[:, :], ACT.Copy, scale=lnw[:, 1, k:k + 1]).then_inc(sd_hi, 1)
                elif w == "logits":
                    act.wait_ge(sd_ready, ready)
                    act.activation(lg[:, :], side[0:NR, :], ACT.Copy).then_inc(sd_read, 1)
                elif w == "softmax":
                    act.wait_ge(lt_done, c + 1)
                    act.activation(rt["e"][:, :, :], rt["d"][:, :, :], ACT.Exp)
                    act.activation(sg[:, :], lt[:, :, NEXP], ACT.Tanh, scale=0.5).then_inc(rt_exp, 1)
                elif w == "turn_comb":
                    act.wait_ge(sd_ready, ready)
                    act.activation(combt[0:32, c % 2, :], side[:, :].bitcast(BF16)[0:32, 0:CH], ACT.Copy).then_inc(sd_read, 1)
                elif w == "y_copy":
                    act.wait_ge(y_used, NIC * (c + 1))
                    act.wait_ge(res_x1, min(c + 2, NCH))
                    act.wait_ge(hn_ready, min(c + 2, NCH))
                    for f in range(2):
                        last = act.activation(x1[:, 2 * f:2 * f + 2, :].rearrange("p a n -> p (a n)"), py[f][:, :], ACT.Copy)
                    last.then_inc(y_read, 1)

            ahead = 0
            for at, w, c in SIDE:
                if at < 0:
                    side_act(w, c)
                    if ahead < 6:
                        split_weights(ahead)
                        ahead += 1
            for n in range(M3 + 4):
                if n < M3:
                    act.wait_ge(g_ready, n + 1)
                    if n >= 2:
                        act.wait_ge(act_step, 3 * (n - 2) + 1)
                    act.activation(th[:, n % 2, :], pg[n % 2][:, :], ACT.Tanh, scale=0.5).then_inc(th_ready, 1)
                    if ahead < NIC:
                        split_weights(ahead)
                        ahead += 1
                    act.wait_ge(act_step, 3 * n + 3)
                    if n >= 2:
                        act.wait_ge(y_used, n - 1)
                    act.activation(act_h[:, n % 2, :], act_f[:, n % 2, :], ACT.Copy).then_inc(ah_ready, 1)
                run_side(n, side_act)

        @block.vector
        def _(dve):
            dve.memset(zb[:, :], 0.0)
            for c in range(NCH):
                dve.wait_ge(x_in, 16 * (c + 1))
                for t in range(4 * c, 4 * c + 4):
                    last = dve.bn_stats(bst[:, t, :], res[:, t, :])
                last.then_inc(bn, 1)
                dve.wait_ge(bn, c + 1)
                for t in range(4 * c, 4 * c + 4):
                    last = dve.bn_aggr(mv[:, t, :], bst[:, t, :])
                last.then_inc(stats, 1)
                if c == 0:
                    dve.wait_ge(w_in, 16)
                    dve.wait_ge(b_in, 32)
                    for cols in (slice(0, CH), slice(CH, CH + D)):
                        for k in range(KC):
                            last = dve.tensor_scalar(wraw[:, k, cols], wraw[:, k, cols], lnw[:, 0, k:k + 1], None, ALU.mult)
                        last.then_inc(w_scaled, 1)
                    dve.wait_ge(c_in, 16)
                    dve.tensor_copy(identb[:, :], ident)
                    dve.tensor_copy(mmaxb[:, :], cst[:, C_MMAX:C_MMAX + P])
                    dve.tensor_copy(mstb[:, :], cst[:, C_MST:C_MST + P]).then_inc(cst_bf, 1)
                    for n in range(3):
                        dve.wait_ge(w_hi, n + 1)
                        w = slice(n * CH, (n + 1) * CH)
                        dve.tensor_tensor(wl[:, :, w], wraw[:, :, w], wh[:, :, w].bitcast(F32), ALU.subtract).then_inc(w_lo, 1)

            def normalise(t, par):
                dve.wait_ge(rs_ln, t + 1)
                if at_least(t, 2):
                    dve.wait_ge(tp_ready, t - 1)
                for dst in (xnp[:, par, :], xn[:, bass.ds(t, 1), :].rearrange("p a d -> p (a d)")):
                    last = dve.tensor_scalar(dst, res[:, bass.ds(t, 1), :].rearrange("p a d -> p (a d)"),
                                             mv[:, bass.ds(t, 1), 0], rstd[:, bass.ds(t, 1)], ALU.subtract, ALU.mult)
                last.then_inc(xn_done, 1)

            def lo_of_x(t, par):
                dve.wait_ge(x_hi, t + 1)
                if at_least(t, 2):
                    dve.wait_ge(mm_ka, t - 1)
                dve.tensor_tensor(xl[:, par, :, :], tp[:, 0:KC * P].rearrange("p (k n) -> p k n", k=KC),
                                  xh[:, par, :, :].bitcast(F32), ALU.subtract).then_inc(x_lo, 1)

            def lo_of_q(m, par):
                t = 2 * m + par
                dve.wait_ge(q_hi, t + 1)
                dve.tensor_tensor(stl[:, par, :, :], qt[:, :, :], sth[:, par, :, :].bitcast(F32), ALU.subtract).then_inc(q_lo, 1)

            normalise(0, 0)
            normalise(1, 1)
            lo_of_x(0, 0)

            def step(m, par):
                t = 2 * m + par
                if at_most(t, NT - 3):
                    normalise(t + 2, par)
                if at_most(t, NT - 2):
                    lo_of_x(t + 1, 1 - par)
                dve.wait_ge(biased, t + 1)
                cs_t = cst[:, bass.ds(C_COS + t * 16, 16)].rearrange("p (q e) -> p q e", q=2)
                if at_least(t, 2):
                    dve.wait_ge(roped, t - 1)
                dve.tensor_tensor(rt1[:, par, :].rearrange("p (q f e) -> p q f e", q=2, e=8),
                                  qksb[:, par, :].rearrange("p (q f e) -> p q f e", q=2, e=8),
                                  cs_t.unsqueeze(2).broadcast_to([P, 2, 2 * H, 8]), ALU.mult).then_inc(rot_cos, 1)
                dve.wait_ge(rot_cos, t + 1)
                dve.wait_ge(rot_sin, t + 1)
                if at_least(t, 2):
                    dve.wait_ge(qt_ready, t - 1)
                dve.tensor_tensor(qkr[:, par, :], rt1[:, par, :], rt2[:, par, :], ALU.add).then_inc(roped, 1)
                if at_least(t, 1):
                    if par:
                        lo_of_q(m, 0)
                    else:
                        lo_of_q(m - 1, 1)

            tiles(dve, step)
            lo_of_q(NT // 2 - 1, 1)
            dve.wait_ge(mm_ka, NT)
            dve.wait_ge(v_done, NT)
            dve.wait_ge(sx_out, 16)
            for i in range(2):
                dve.wait_ge(sa_out[i], 16 * (NT // 2))
                dve.wait_ge(sq_out[i], 32 * (NT // 2))

            dve.memset(alog[:, :, :], 0.0).then_inc(a_sum, 1)

            def take_max(i):
                u, r, pairs, e, k0, w, _ = PIECES[i]
                dve.wait_ge(mx_ready, i + 1)
                if u >= 2:
                    dve.wait_ge(nm_step, 2 * (u - 2) + 1)
                dve.tensor_reduce(mxp[:, u % 2, r, pairs[0]:pairs[-1] + 1, e, k0 // CH],
                                  mx[BANK_AT["piece", i] % 3][:, 0:w * len(pairs)].rearrange("p (s k) -> p s k", k=w),
                                  AX.X, ALU.max).then_inc(mx_read, 1)

            def negate(u):
                c = UNITS[u][1]
                dve.wait_ge(mx_read, PIECE_END[u])
                if u >= 1:
                    dve.wait_ge(nm_ready, u)
                dve.tensor_reduce(nmx[:, :, :, :], mxp[:, u % 2, :, :, :, 0:c + 1], AX.X, ALU.max, negate=True).then_inc(nm_step, 1)
                dve.wait_ge(nm_step, 2 * u + 1)
                if u >= 2:
                    dve.wait_ge(nt_ready, u - 1)
                dst = nmt[:, u % 2, :, :].rearrange("p r (e a s) -> p r e a s", e=2, a=2)
                src = nmx[:, :, :, :].rearrange("p r s e -> p r e s")
                dve.tensor_copy(dst[:, :, :, 0, :], src).then_inc(nm_step, 1)
                dve.wait_ge(nm_step, 2 * u + 2)
                dve.tensor_tensor(dst[:, :, :, 1, :], src, dst[:, :, :, 0, :].bitcast(F32), ALU.subtract).then_inc(nm_ready, 1)

            def context(u):
                dve.wait_ge(ot_ready, u + 1)
                if u >= 1:
                    dve.wait_ge(ctx_ready, u)
                ov = mx[BANK_AT["ctx", u] % 3][:, :].rearrange("p (r j d) -> p r j d", r=CH // P, j=G)
                dve.reciprocal(orec[:, :, :], ov[:, :, :, HD]).then_inc(o_rec, 1)
                dve.wait_ge(o_rec, u + 1)
                if u >= 2:
                    dve.wait_ge(ctx_out[u % 2], 16 * (u // 2))
                dve.tensor_tensor(ctxs[:, u % 2, :, :].rearrange("p r (j d) -> p r j d", j=G), ov[:, :, :, 0:HD],
                                  orec[:, :, :].unsqueeze(3).broadcast_to([P, CH // P, G, HD]),
                                  ALU.mult).then_inc(ctx_ready, 1)

            def over_heads(kind, t):
                if kind < 4:
                    if kind == 0:
                        dve.wait_ge(a_prod, t + 1)
                        if t >= 1:
                            dve.wait_ge(a_masked, t)
                        else:
                            dve.wait_ge(a_sum, 1)
                    ins = dve.tensor_reduce(alog[:, 4 * kind:4 * kind + 4, 0:4 * (kind + 1)], qkp[kind][:, :, :, :], AX.X, ALU.add)
                    if kind == 3:
                        ins.then_inc(a_log, 1)
                elif kind == MAXIMA:
                    dve.wait_ge(a_masked, t + 1)
                    dve.tensor_reduce(amx[:, :], amask[:, :, :], AX.X, ALU.max).then_inc(a_max, 1)
                elif kind == SUMS:
                    dve.wait_ge(a_exp, t + 1)
                    if t >= 1:
                        dve.wait_ge(a_rec, t)
                    dve.tensor_reduce(asum[:, :], aexp[:, :, :], AX.X, ALU.add).then_inc(a_sum, 1)
                    dve.wait_ge(a_sum, t + 2)
                    if t >= 1:
                        dve.wait_ge(a_done, t)
                    dve.reciprocal(arec[:, :], asum[:, :]).then_inc(a_rec, 1)

            def read_banks(s, gap):
                for kind, n in BANK_PLAN[s, gap]:
                    if kind == "piece":
                        take_max(n)
                        if n + 1 in PIECE_END:
                            negate(PIECE_END.index(n + 1))
                    elif kind == "ctx":
                        context(n)

            read_banks(-1, 0)
            for s in range(NS + 2):
                read_banks(s, 0)
                read_banks(s, 1)
                for kind, t in a_steps.get(s, []):
                    if kind != EXPS:
                        over_heads(kind, t)
                read_banks(s, 2)

            dve.wait_ge(ctx_ready, NU)
            dve.sem_inc(att_end, 1)
            dve.wait_ge(att_end, 4)
            dve.memset(combt[:, :, :], 0.0)
            dve.memset(cbt[:, :, :], 0.0).then_inc(c3_set, 1)

            steps = [0]

            def small(ins):
                ins.then_inc(rt_step, 1)
                steps[0] += 1
                dve.wait_ge(rt_step, steps[0])

            def side_dve(w, c):
                if w in BANKED:
                    use = side_use[w, c]
                if w in ("turn_ctx0", "turn_ctx1"):
                    k = int(w[-1])
                    dve.wait_ge(sd_hi, 4 * c + k + 1)
                    dve.tensor_tensor(ctl[:, k, :], side[:, :], cth[:, k, :].bitcast(F32), ALU.subtract).then_inc(sd_read, 1)
                elif w in ("proj_a", "proj_b"):
                    r = slice(0, 2) if w == "proj_a" else slice(2, 4)
                    dve.wait_ge(sd_ready, use + 1)
                    dve.wait_ge(xr_in, 16 * (c + 1))
                    if c >= 1:
                        dve.wait_ge(res_x1, c)
                    if c >= 2:
                        dve.wait_ge(sd_ready, side_use["out_b", c - 2] + 1)
                    dve.tensor_tensor(x1[:, r, :], side[:, :].rearrange("p (r n) -> p r n", r=2), xin[:, r, :],
                                      ALU.add).then_inc(sd_read, 1)
                    if w == "proj_b":
                        dve.wait_ge(sd_read, use + 1)
                        if c >= 1:
                            dve.wait_ge(r2_ready, c)
                        for i in range(4):
                            if c or i:
                                dve.wait_ge(x1_ready, 4 * c + i)
                            dve.tensor_tensor_reduce(sqj[:, :], x1[:, i, :], x1[:, i, :], 1.0, 0.0, ALU.mult, ALU.add,
                                                     msq[:, i:i + 1]).then_inc(x1_ready, 1)
                        dve.wait_ge(x1_ready, 4 * c + 4)
                        dve.sem_inc(sq_done, 1)
                elif w == "normalise":
                    dve.wait_ge(r2_ready, c + 1)
                    for i in range(4):
                        last = dve.tensor_scalar(ctxin[:, i, :], x1[:, i, :], rms2[:, i:i + 1], None, ALU.mult)
                    last.then_inc(hn_ready, 1)
                elif w in ("turn_h0", "turn_h1"):
                    k = int(w[-1])
                    dve.wait_ge(sd_hi, 4 * c + 2 + k + 1)
                    dve.scalar_tensor_tensor(out=htl[:, c % 2, k, :], in0=side[:, :], scalar=lnw[:, 1, k:k + 1],
                                             in1=hth[:, c % 2, k, :].bitcast(F32), op0=ALU.mult, op1=ALU.subtract).then_inc(sd_read, 1)
                elif w == "turn_logits":
                    dve.wait_ge(sd_ready, use + 1)
                    if c >= 1:
                        dve.wait_ge(cb_ready, c)
                    dve.tensor_copy(lt[:, :, :], side[:, 0:64].rearrange("p (r n) -> p r n", r=4)[:, :, 0:NR]).then_inc(sd_read, 1)
                    dve.wait_ge(sd_read, use + 1)
                    small(dve.tensor_reduce(rs4["mx"][:, :], lt[:, :, 0:NEXP], AX.X, ALU.max))
                    dve.tensor_tensor(rt["d"][:, :, :], lt[:, :, 0:NEXP], rs4["mx"][:, :].unsqueeze(2).broadcast_to([P, 4, NEXP]),
                                      ALU.subtract).then_inc(lt_done, 1)
                elif w == "top2":
                    dve.wait_ge(rt_exp, c + 1)
                    wide = lambda a: a[:, :].unsqueeze(2).broadcast_to([P, 4, NEXP])
                    key = cst[:, C_KEY:C_KEY + NEXP].unsqueeze(1).broadcast_to([P, 4, NEXP])
                    small(dve.tensor_reduce(rs4["sum"][:, :], rt["e"][:, :, :], AX.X, ALU.add))
                    small(dve.reciprocal(rs4["rec"][:, :], rs4["sum"][:, :]))
                    small(dve.tensor_tensor(rt["p"][:, :, :], rt["e"][:, :, :], wide(rs4["rec"]), ALU.mult))
                    for src, m, k, oh in (("p", "m1", "k1", "oh1"), ("p2", "m2", "k2", "oh2")):
                        small(dve.tensor_reduce(rs4[m][:, :], rt[src][:, :, :], AX.X, ALU.max))
                        small(dve.tensor_tensor(rt["is"][:, :, :], rt[src][:, :, :], wide(rs4[m]), ALU.is_equal))
                        small(dve.tensor_tensor(rt["key"][:, :, :], rt["is"][:, :, :], key, ALU.mult))
                        small(dve.tensor_reduce(rs4[k][:, :], rt["key"][:, :, :], AX.X, ALU.max))
                        small(dve.tensor_tensor(rt[oh][:, :, :], rt["key"][:, :, :], wide(rs4[k]), ALU.is_equal))
                        if src == "p":
                            small(dve.scalar_tensor_tensor(out=rt["p2"][:, :, :], in0=rt["oh1"][:, :, :], scalar=-4.0,
                                                           in1=rt["p"][:, :, :], op0=ALU.mult, op1=ALU.add))
                    small(dve.tensor_tensor(rt["oh"][:, :, :], rt["oh1"][:, :, :], rt["oh2"][:, :, :], ALU.add))
                    small(dve.scalar_tensor_tensor(out=cw[:, :, 0:NEXP], in0=rt["oh"][:, :, :], scalar=0.5, in1=rt["p"][:, :, :],
                                                   op0=ALU.mult, op1=ALU.mult))
                    small(dve.tensor_scalar(cw[:, :, NEXP], sg[:, :], 0.25, 0.25, ALU.mult, ALU.add))
                    if c >= 1:
                        dve.wait_ge(sd_ready, side_use["turn_comb", c - 1] + 1)
                    small(dve.tensor_copy(cbt[:, :, 0:NR], cw[:, :, :]))
                    small(dve.tensor_tensor(cwr[:, 0, :, :], cw[:, :, :], cbt[:, :, 0:NR], ALU.subtract))
                    small(dve.tensor_copy(cbt[:, :, NR:2 * NR], cwr[:, 0, :, :]))
                    small(dve.tensor_tensor(cwr[:, 1, :, :], cwr[:, 0, :, :], cbt[:, :, NR:2 * NR], ALU.subtract))
                    dve.tensor_copy(cbt[:, :, 2 * NR:3 * NR], cwr[:, 1, :, :]).then_inc(cb_ready, 1)
                elif w in ("out_a", "out_b"):
                    t2 = slice(4 * c + 2 * (w == "out_b"), 4 * c + 2 * (w == "out_b") + 2)
                    dve.wait_ge(sd_ready, use + 1)
                    dve.wait_ge(res_x1, c + 1)
                    dve.tensor_tensor(res[:, t2, :], res[:, t2, :], side[:, :].rearrange("p (r n) -> p r n", r=2),
                                      ALU.add).then_inc(sd_read, 1)
                    dve.wait_ge(sd_read, use + 1)
                    dve.sem_inc(out_ready, 1)

            run_side(-1, side_dve)
            for n in range(M3 + 4):
                if n < M3:
                    dve.wait_ge(th_ready, n + 1)
                    if n >= 2:
                        dve.wait_ge(al_ready, n - 1)
                    dve.scalar_tensor_tensor(out=act_f[:, n % 2, :], in0=th[:, n % 2, :], scalar=1.0, in1=pg[n % 2][:, :],
                                             op0=ALU.add, op1=ALU.mult).then_inc(act_step, 1)
                    dve.wait_ge(act_step, 3 * n + 1)
                    dve.wait_ge(u_ready, n + 1)
                    dve.tensor_tensor(act_f[:, n % 2, :], act_f[:, n % 2, :], pu[n % 2][:, :], ALU.mult).then_inc(act_step, 1)
                    dve.wait_ge(act_step, 3 * n + 2)
                    dve.wait_ge(c_ready, n + 1)
                    dve.tensor_tensor(act_f[:, n % 2, :], act_f[:, n % 2, :], pc[:, :], ALU.mult).then_inc(act_step, 1)
                run_side(n, side_dve)
                if n < M3:
                    dve.wait_ge(ah_ready, n + 1)
                    dve.tensor_tensor(act_l[:, n % 2, :], act_f[:, n % 2, :], act_h[:, n % 2, :].bitcast(F32),
                                      ALU.subtract).then_inc(al_ready, 1)

        @block.tensor
        def _(pe):
            def three(dst, a_hi, a_lo, b_hi, b_lo, k):
                pe.matmul(dst, a_hi, b_hi, start=(k == 0), stop=False)
                pe.matmul(dst, a_hi, b_lo, start=False, stop=False)
                return pe.matmul(dst, a_lo, b_hi, start=False, stop=(k == KC - 1))

            def turn_x(t, par):
                pe.wait_ge(xn_done, t + 1)
                if at_least(t, 1):
                    pe.wait_ge(x_lo, t)
                for k in range(KC):
                    last = pe.transpose(tp[:, k * P:(k + 1) * P], xnp[:, par, k * P:(k + 1) * P], ident)
                last.then_inc(tp_ready, 1)

            def turn_q(t, par):
                pe.wait_ge(roped, t + 1)
                if at_least(t, 1):
                    pe.wait_ge(q_lo, t)
                for f in range(4):
                    last = pe.transpose(qt[:, f, :], qkr[:, par, f * P:(f + 1) * P], ident)
                last.then_inc(qt_ready, 1)

            pe.wait_ge(c_in, 16)
            turn_x(0, 0)

            def step(m, par):
                t = 2 * m + par
                if at_most(t, NT - 2):
                    turn_x(t + 1, 1 - par)
                pe.wait_ge(x_lo, t + 1)
                if at_least(t, 2):
                    pe.wait_ge(e_a, t - 1)
                for n, (dst, done) in enumerate(((pqk, mm_qk), (pva, mm_va), (pka, mm_ka))):
                    if isinstance(t, int) and t == 0:
                        pe.wait_ge(w_lo, n + 1)
                    w = slice(n * CH, (n + 1) * CH)
                    for k in range(KC):
                        last = three(dst[par][:, :], xh[:, par, k, :], xl[:, par, k, :], wh[:, k, w], wl[:, k, w], k)
                    last.then_inc(done, 1)
                if at_least(t, 1):
                    turn_q(t - 1, 1 - par)

            tiles(pe, step)
            turn_q(NT - 1, 1)
            pe.wait_ge(q_lo, NT)
            pe.wait_ge(e_a, NT)
            pe.wait_ge(cst_bf, 1)
            pe.wait_ge(v_ones, 1)
            pe.wait_ge(v_done, NT)

            def max_piece(i, bank):
                u, r, pairs, e, k0, w, diagonal = PIECES[i]
                g, c = UNITS[u]
                if i == 0 or UNITS[PIECES[i - 1][0]][0] != g:
                    pe.wait_ge(stk_in[g % 2], 16 * 12 * (g // 2 + 1))
                q0 = c * CH + r * P
                for n, pair in enumerate(pairs):
                    last = pe.matmul(bank[:, n * w:(n + 1) * w], qs[g % 2][0:2 * KROWS, pair, e, q0:q0 + P],
                                     ks[g % 2][0:2 * KROWS, pair, k0:k0 + w], start=True, stop=not diagonal)
                    if diagonal:
                        last = pe.matmul(bank[:, (n + 1) * w - P:(n + 1) * w], identb[:, :], mmaxb[:, :],
                                         start=False, stop=True)
                last.then_inc(mx_ready, 1)

            def bank_use(kind, n):
                at = BANK_AT[kind, n]
                bank = mx[at % 3]
                if at >= 3:
                    k, i = BANK_USES[at - 3]
                    pe.wait_ge({"piece": mx_read, "neg": nr_ready, "ctx": ctx_ready}[k], i + 1)
                if kind == "piece":
                    max_piece(n, bank)
                elif kind == "neg":
                    pe.wait_ge(nm_ready, n + 1)
                    for r in range(CH // P):
                        last = pe.transpose(bank[0:8, r * P:(r + 1) * P], nmt[:, n % 2, r, :].bitcast(F32), ident)
                    last.then_inc(nt_ready, 1)
                else:
                    pe.wait_ge(o_read, n + 1)
                    for r in range(CH // P):
                        last = pe.transpose(bank[:, r * P:(r + 1) * P], osb[:, r * P:(r + 1) * P], ident)
                    last.then_inc(ot_ready, 1)

            def bank_uses(s, gap):
                for use in BANK_PLAN[s, gap]:
                    bank_use(*use)

            def scores(s, pr):
                u, kb = STEPS[s]
                g, c = UNITS[u]
                off = first_key_column(s)
                if s >= 1:
                    pe.wait_ge(exped, 2 * s + pr - 1)
                for e in range(2):
                    diagonal = kb * P >= c * CH
                    last = pe.matmul(st[pr][:, e, off:CH], ks[g % 2][:, pr, kb * P:(kb + 1) * P],
                                     qs[g % 2][:, pr, e, c * CH + off:(c + 1) * CH], start=True, stop=not diagonal)
                    if diagonal:
                        last = pe.matmul(st[pr][:, e, off:off + P], identb[:, :], mstb[:, :], start=False, stop=True)
                last.then_inc(st_ready, 1)

            def weigh(s):
                u, kb = STEPS[s]
                g, c = UNITS[u]
                off = first_key_column(s)
                pe.wait_ge(exped, 2 * s + 2)
                if kb == 0 and u >= 1:
                    pe.wait_ge(o_read, u)
                for j in range(G):
                    last = pe.matmul(o[32 * j:32 * j + VC, off:CH], v[:, kb, 4 * g + j, :],
                                     pt[:, s % 2, j // 2, j % 2, off:CH], start=(kb == 0), stop=(kb == 4 * c + 3))
                last.then_inc(av_done, 1)

            def before_scores(s):
                u, kb = STEPS[s]
                if kb == 0:
                    pe.wait_ge(nr_in[u % 4], 32 * (u // 4 + 1))

            pe.matmul(o[:, :], zb[:, 0:P], zb[:, :], start=True, stop=True).then_inc(o_zero, 1)
            bank_uses(-1, 0)
            before_scores(0)
            scores(0, 0)
            scores(0, 1)
            for s in range(NS + 2):
                if s < NS - 1:
                    before_scores(s + 1)
                    scores(s + 1, 0)
                bank_uses(s, 0)
                if s < NS - 1:
                    scores(s + 1, 1)
                bank_uses(s, 1)
                if s < NS:
                    weigh(s)
                bank_uses(s, 2)

            pe.wait_ge(ctx_ready, NU)
            pe.sem_inc(att_end, 1)
            pe.wait_ge(att_end, 4)

            def side_pe(w, c):
                if w not in BANKED:
                    return
                use = side_use[w, c]
                if use:
                    pe.wait_ge(sd_read, use)
                if w in ("turn_ctx0", "turn_ctx1", "turn_h0", "turn_h1"):
                    k = int(w[-1])
                    if w.startswith("turn_ctx"):
                        pe.wait_ge(cx_in, 16 * (c + 1))
                    else:
                        pe.wait_ge(hn_ready, c + 1)
                    for r in range(4):
                        last = pe.transpose(side[:, r * P:(r + 1) * P], ctxin[:, r, k * P:(k + 1) * P], ident)
                elif w in ("proj_a", "proj_b"):
                    pe.wait_ge(ws_lo, 2)
                    for r in range(2):
                        tok = slice((2 * (w == "proj_b") + r) * P, (2 * (w == "proj_b") + r + 1) * P)
                        for k in range(KC):
                            last = three(side[:, r * D:(r + 1) * D], cth[:, k, tok], ctl[:, k, tok], woh[:, k, :], wol[:, k, :], k)
                elif w == "logits":
                    for k in range(KC):
                        last = three(side[0:NR, :], wrh[:, k, :], wrl[:, k, :], hth[:, c % 2, k, :], htl[:, c % 2, k, :], k)
                elif w == "turn_logits":
                    for r in range(4):
                        last = pe.transpose(side[:, 16 * r:16 * r + NR], lg[:, r * P:(r + 1) * P], cst[0:NR, C_ID:C_ID + NR])
                elif w == "turn_comb":
                    pe.wait_ge(cb_ready, c + 1)
                    for r in range(4):
                        last = pe.transpose(side[:, :].bitcast(BF16)[0:32, r * P:(r + 1) * P], cbt[:, r, :], identb[:, :])
                else:
                    pe.wait_ge(y_read, c + 1)
                    for i in range(2):
                        r = 2 * (w == "out_b") + i
                        for f in range(2):
                            y = x1[:, 2 * f:2 * f + 2, :].rearrange("p a n -> p (a n)")
                            last = pe.transpose(side[:, i * D + f * P:i * D + (f + 1) * P], y[:, r * P:(r + 1) * P], ident)
                last.then_inc(sd_ready, 1)

            def down(n):
                c, ic = divmod(n, NIC)
                pe.wait_ge(al_ready, n + 1)
                if ic == 0 and c >= 1:
                    pe.wait_ge(y_read, c)
                for f in range(2):
                    for i, (a, b) in enumerate(((mh, act_h), (mh, act_l), (ml, act_h))):
                        last = pe.matmul(py[f][:, :], a[ic][:, 4 + f, :], b[:, n % 2, :],
                                         start=(ic == 0 and i == 0), stop=(ic == NIC - 1 and i == 2))
                last.then_inc(y_used, 1)

            run_side(-1, side_pe)
            pe.wait_ge(sel_in, 16)
            pe.wait_ge(c3_set, 1)
            for n in range(M3 + 4):
                c, ic = divmod(n, NIC)
                if 2 <= n < M3 + 2:
                    down(n - 2)
                if n < M3:
                    if c == 0:
                        pe.wait_ge(m_lo, ic + 1)
                    if n >= 2:
                        pe.wait_ge(act_step, 3 * (n - 2) + 2)
                    for dst, at, done in ((pg, 0, g_ready), (pu, 2, u_ready)):
                        for k in range(KC):
                            last = three(dst[n % 2][:, :], mh[ic][:, at + k, :], ml[ic][:, at + k, :],
                                         hth[:, c % 2, k, :], htl[:, c % 2, k, :], k)
                        last.then_inc(done, 1)
                    if ic == 0:
                        pe.wait_ge(sd_read, side_use["turn_comb", c] + 1)
                    if n >= 1:
                        pe.wait_ge(act_step, 3 * (n - 1) + 3)
                    pe.matmul(pc[:, :], selb[:, ic * P:(ic + 1) * P], combt[:, c % 2, :], start=True, stop=True).then_inc(c_ready, 1)
                run_side(n, side_pe)


def kernel(**inputs):
    import numpy as np
    import concourse.bacc as bacc
    from concourse.bass_utils import run_bass_kernel_spmd

    a = {n: np.asarray(v) for n, v in inputs.items()}
    f = {n[len("L0_ffn_"):]: v for n, v in a.items() if n.startswith("L0_ffn_")}
    wide = lambda w: w.transpose(1, 0, 2).reshape(D, -1)
    pad = NIC * P - I_ALL
    gate = np.pad(np.concatenate([wide(f["w_gate_e"]), f["w_sh_gate"]], 1), ((0, 0), (0, pad)))
    up = np.pad(np.concatenate([wide(f["w_up_e"]), f["w_sh_up"]], 1), ((0, 0), (0, pad)))
    down = np.pad(np.concatenate([f["w_down_e"].reshape(-1, D), f["w_sh_down"]], 0), ((0, pad), (0, 0)))
    split = lambda w: w.reshape(KC, P, NIC, P).transpose(2, 1, 0, 3).reshape(NIC, P, KC * P)
    arrays = {
        "x": a["L0_attn_input_seq_embs"][0],
        "wproj": np.concatenate([f["wq"], f["wk"], f["wv"]] + [a[f"L0_attn_W{n}"].T for n in "qkv"], 1),
        "bqkv": np.concatenate([f["bq"], f["bk"], f["bv"]]),
        "wln": np.stack([f["w_ln1"], f["w_ln2"]]).reshape(2, KC, P).transpose(2, 0, 1),
        "wo": f["wo"],
        "wr": np.concatenate([f["w_router"], f["w_sh_eg"]], 1),
        "wmoe": np.concatenate([split(gate), split(up), down.reshape(NIC, P, D)], 2),
    }
    pos = np.arange(T, dtype=np.float32).reshape(NT, P).T
    inv = (1.0 / THETA ** (np.arange(0, HD, 2, dtype=np.float32) / HD)).astype(np.float32)
    ang = pos[:, :, None] * inv
    cos, sin = np.cos(ang), np.sin(ang)
    row, col = np.arange(P)[:, None], np.arange(P)[None, :]
    heads = np.where(np.arange(H)[None, :] > np.arange(H)[:, None], NEG, 0.0).reshape(1, -1)
    scale = HD ** -0.5
    consts = np.concatenate([
        np.eye(P), np.where(col > row, NEG, 0.0), np.where(col < row, NEG, 0.0), np.repeat(heads, P, 0),
        np.stack([cos * scale, cos], 2).reshape(P, -1),
        np.stack([np.stack([-sin, sin], 2) * scale, np.stack([-sin, sin], 2)], 2).reshape(P, -1),
        np.repeat(np.arange(NEXP, 0, -1)[None, :], P, 0),
    ], 1).astype(np.float32)
    owner = np.minimum(np.arange(NIC * P) // MOE_I, NEXP)
    sel = np.tile((owner[None, :] == np.arange(NR)[:, None]).astype(np.float32), (3, 1))
    arrays["consts"], arrays["sel"] = consts, sel

    nc = bacc.Bacc("TRN2", target_bir_lowering=False, num_devices=1)
    arrays = {n: np.ascontiguousarray(v) for n, v in arrays.items()}
    io = {n: nc.dram_tensor(n, v.shape, mybir.dt.from_np(v.dtype), kind="ExternalInput").ap() for n, v in arrays.items()}
    io["out"] = nc.dram_tensor("out", (T, D), F32, kind="ExternalOutput").ap()
    for name, shape in (("sq", (2, 2 * D, T)), ("sa", (NT, P, 3 * D)), ("sx", (P, NT, D)), ("sn", (NU, 8, CH)), ("sc", (P, NT, D))):
        io[name] = nc.dram_tensor(name, shape, F32, kind="Internal").ap()
    block_program(nc, **io)
    r = run_bass_kernel_spmd(nc, [arrays], core_ids=[0])
    return r.results[0]["out"].reshape(1, T, D)
```

```python
from contextlib import ExitStack

import concourse.bass as bass
from concourse import mybir

P = 128
T, D = 2048, 256
H, HD = 16, 16
NT = T // P
CH = 512
NCH = T // CH
KC = D // P
G = 4
NG = H // G
NEXP, MOE_I, SH_I = 8, 176, 704
I_ALL = NEXP * MOE_I + SH_I
NIC = -(-I_ALL // P)
NR = NEXP + 1
LN_EPS, RMS_EPS = 1e-5, 1e-6
THETA = 1000000.0
NEG = -1e30
VC = HD + 1
FIRST_COLS = 2 * CH
KROWS = 3 * HD

F32 = mybir.dt.float32
F32R = mybir.dt.float32r
BF16 = mybir.dt.bfloat16
ALU = mybir.AluOpType
ACT = mybir.ActivationFunctionType
AX = mybir.AxisListType

C_ID, C_MMAX, C_MST, C_MA = 0, 128, 256, 384
C_COS = C_MA + H * H
C_SIN = C_COS + NT * 16
C_KEY = C_SIN + NT * 32
C_ALL = C_KEY + NEXP


UNITS = [(g, c) for g in range(NG) for c in (range(NCH) if g < NG - 1 else reversed(range(NCH)))]
NU = len(UNITS)


def score_pieces():
    out = []
    for u, (g, c) in enumerate(UNITS):
        for r in range(CH // P):
            keys = P * (CH // P * c + r + 1)
            for b in range(-(-keys // CH)):
                w = min(CH, keys - b * CH)
                diagonal = (b + 1) * CH >= keys
                for pairs in ([[0, 1]] if 2 * w <= CH else [[0], [1]]):
                    for e in range(2):
                        out.append((u, r, pairs, e, b * CH, w, diagonal))
    return out


PIECES = score_pieces()
STEPS = [(u, kb) for u, (g, c) in enumerate(UNITS) for kb in range(CH // P * (c + 1))]
NS = len(STEPS)
UNIT_FIRST = [STEPS.index((u, 0)) for u in range(NU)]
UNIT_LAST = [s - 1 for s in UNIT_FIRST[1:]] + [NS - 1]
PIECE_END = [max(i for i, p in enumerate(PIECES) if p[0] == u) + 1 for u in range(NU)]
GAPS, LEAD = 3, 6


def first_key_column(s):
    u, kb = STEPS[s]
    return max(0, kb * P - UNITS[u][1] * CH)


def pieces_by_gap():
    cost = [p[5] * len(p[2]) + 100 for p in PIECES]
    share = [0.36, 0.28, 0.36]
    given = [[0] * GAPS for _ in range(NS)]
    i, owed = len(PIECES), 0.0
    for s in reversed(range(NS)):
        for gap in reversed(range(GAPS)):
            given[s][gap] = i
            owed += RATE * share[gap] * 4 * (CH - first_key_column(s))
            while i and (owed > 0):
                if s > UNIT_FIRST[PIECES[i - 1][0]] - LEAD:
                    owed = min(owed, 0.0)
                    break
                i -= 1
                owed -= cost[i]
    return i, given


RATE = 1.2
AHEAD, GIVEN = pieces_by_gap()
STACKS_FREE = UNIT_LAST[(NG - 1) * NCH - 1] + 1
MAX_STEP = [-1 if AHEAD >= e else next(s for s in range(NS) if GIVEN[s][-1] >= e) for e in PIECE_END]
SLICES_AHEAD = 3
SPLIT_AT = [NS - 8, NS - 6, NS]
SLICE_OVER_A = 11
EARLY_AFTER = 6
EARLY_WORK = {0: "turn_ctx0", 1: "turn_ctx1", 2: "proj_a", 3: "proj_b", 6: "normalise", 7: "turn_h0", 8: "turn_h1",
              10: "logits", 11: "turn_logits", 12: "softmax", 13: "largest", 14: "second",
              15: "combine"}
TURNS = {}
for u in range(NU):
    TURNS.setdefault(MAX_STEP[u] + 1 if MAX_STEP[u] >= 0 else -1, []).append(("neg", u))
for u in range(NU):
    TURNS.setdefault(UNIT_LAST[u] + 1, []).append(("ctx", u))


EARLY_AT = UNIT_LAST[NU - NCH] + EARLY_AFTER
EARLY = {EARLY_AT + at: w for at, w in EARLY_WORK.items()}
BANKED = ("turn_ctx0", "turn_ctx1", "proj_a", "proj_b", "turn_h0", "turn_h1", "logits", "turn_logits",
          "turn_comb", "out_a", "out_b")
EARLY_BANKED = [w for s, w in sorted(EARLY.items()) if w in BANKED]


def bank_plan():
    plan, done = {}, 0

    def give(place, upto):
        nonlocal done
        plan.setdefault(place, []).extend(("piece", i) for i in range(done, upto))
        done = max(done, upto)

    for turn in TURNS.get(-1, []):
        give((-1, 0), min(PIECE_END[turn[1]] + 2, AHEAD))
        plan[-1, 0].append(turn)
    give((-1, 0), AHEAD)
    for s in range(NS + 2):
        for gap in range(GAPS):
            give((s, gap), GIVEN[s][gap] if s < NS else done)
        plan[s, GAPS - 1] += TURNS.get(s, [])
        if EARLY.get(s) in EARLY_BANKED:
            plan[s, GAPS - 1].append(("side", EARLY_BANKED.index(EARLY[s])))
    return plan


BANK_PLAN = bank_plan()
BANK_USES = [use for place in BANK_PLAN for use in BANK_PLAN[place]]
BANK_AT = {use: n for n, use in enumerate(BANK_USES)}


def block_program(nc, x, wproj, bqkv, wln, wo, wr, wmoe, consts, sel, out, sq, sa, sx, sn, sc, sz):
    xv = x.rearrange("(t p) d -> p t d", p=P)
    outv = out.rearrange("(t p) d -> p t d", p=P)

    with ExitStack() as ctx:
        def sb(name, shape, dt, stack=ctx):
            return stack.enter_context(nc.sbuf_tensor(name, shape, dt))

        def ps(name, shape, dt=F32, stack=ctx):
            return stack.enter_context(nc.psum_tensor(name, shape, dt))

        def sem(name):
            return ctx.enter_context(nc.semaphore(name))

        res = sb("res", [P, NT, D], F32)
        cst = sb("cst", [P, C_ALL], F32)
        identb = sb("identb", [P, P], BF16)
        mmaxb = sb("mmaxb", [P, P], BF16)
        mstb = sb("mstb", [P, P], BF16)
        lnw = sb("lnw", [P, 2, KC], F32)
        bias = sb("bias", [P, 3 * D], F32)
        zb = sb("zb", [P, CH], BF16)
        mraw = sb("mraw", [P, 2, 6, P], F32)
        ident = cst[:, C_ID:C_ID + P]
        mask_a = cst[:, C_MA:C_MA + H * H].rearrange("p (h g) -> p h g", h=H)

        s2 = ExitStack()
        qs = [sb("qs0", [P, 2, 2, T], F32R, s2)]
        ks = [sb("ks0", [P, 2, T], F32R, s2)]
        v = sb("v", [P, NT, H, VC], F32, s2)
        mxp = sb("mxp", [P, 2, CH // P, 2, 2, NCH], F32, s2)
        nmx = sb("nmx", [P, CH // P, 2, 2], F32, s2)
        nmt = sb("nmt", [P, 2, CH // P, 8], F32R, s2)
        nmr = sb("nmr", [8, 2, CH], F32, s2)
        s12 = s2.enter_context(ExitStack())
        qs.append(sb("qs1", [P, 2, 2, T], F32R, s12))
        ks.append(sb("ks1", [P, 2, T], F32R, s12))
        pt = sb("pt", [P, 2, 2, 2, CH], F32, s12)
        ain = sb("ain", [P, 2, 3 * D], F32, s12)
        qkp = [sb(f"qkp{b}", [P, 4, 4 * (b + 1), HD], F32, s12) for b in range(4)]
        avp = [sb(f"avp{b}", [P, 4, 4 * (b + 1), HD], F32, s12) for b in range(4)]
        alog = sb("alog", [P, H, H], F32, s12)
        amask = sb("amask", [P, H, H], F32, s12)
        ashift = sb("ashift", [P, H, H], F32, s12)
        aexp = sb("aexp", [P, H, H], F32, s12)
        amx = sb("amx", [P, H], F32, s12)
        asum = sb("asum", [P, H], F32, s12)
        arec = sb("arec", [P, H], F32, s12)
        aout = sb("aout", [P, H, HD], F32, s12)
        ascl = sb("ascl", [P, H, HD], F32, s12)
        osb = sb("osb", [P, CH], F32, s12)
        orec = sb("orec", [P, CH // P, G], F32, s12)
        ctxs = sb("ctxs", [P, 2, CH // P, G * HD], F32, s12)
        s12.close()
        s1 = ExitStack()
        xn = sb("xn", [P, NT, D], F32, s1)
        wraw = sb("wraw", [P, KC, 6 * D], F32, s1)
        wh = sb("wh", [P, KC, 6 * D], F32R, s1)
        wl = sb("wl", [P, KC, 6 * D], F32R, s1)
        xnp = sb("xnp", [P, 2, D], F32, s1)
        xh = sb("xh", [P, 2, KC, P], F32R, s1)
        xl = sb("xl", [P, 2, KC, P], F32R, s1)
        qksb = sb("qksb", [P, 2, 2 * D], F32, s1)
        vst = sb("vst", [P, 2, D], F32, s1)
        asb = sb("asb", [P, 2, 3 * D], F32, s1)
        rt1 = sb("rt1", [P, 2, 2 * D], F32, s1)
        rt2 = sb("rt2", [P, 2, 2 * D], F32, s1)
        qkr = sb("qkr", [P, 2, 2 * D], F32, s1)
        sth = sb("sth", [P, 2, 4, P], F32R, s1)
        stl = sb("stl", [P, 2, 4, P], F32R, s1)
        bst = sb("bst", [P, NT, 6], F32, s1)
        mv = sb("mv", [P, NT, 2], F32, s1)
        tmpr = sb("tmpr", [P, NT], F32, s1)
        rstd = sb("rstd", [P, NT], F32, s1)
        rms1 = sb("rms1", [P, NT], F32, s1)
        half = sb("half", [P, 4], F32, s1)
        s1.close()
        s2.close()
        s3 = ExitStack()
        woraw = sb("woraw", [P, KC, D], F32, s3)
        woh = sb("woh", [P, KC, D], F32R, s3)
        wol = sb("wol", [P, KC, D], F32R, s3)
        wrraw = sb("wrraw", [P, KC, NR], F32, s3)
        wrh = sb("wrh", [P, KC, NR], F32R, s3)
        wrl = sb("wrl", [P, KC, NR], F32R, s3)
        ctxin = sb("ctxin", [P, 4, D], F32, s3)
        xin = sb("xin", [P, 4, D], F32, s3)
        cth = sb("cth", [P, KC, CH], F32R, s3)
        ctl = sb("ctl", [P, KC, CH], F32R, s3)
        x1 = sb("x1", [P, 4, D], F32, s3)
        sqj = sb("sqj", [P, D], F32, s3)
        hth = sb("hth", [P, 2, KC, CH], F32R, s3)
        htl = sb("htl", [P, 2, KC, CH], F32R, s3)
        lg = sb("lg", [NR, CH], F32, s3)
        cbt = sb("cbt", [P, 4, 32], BF16, s3)
        msq = sb("msq", [P, 4], F32, s3)
        msq1 = sb("msq1", [P, 4], F32, s3)
        rms2 = sb("rms2", [P, 4], F32, s3)
        half3 = sb("half3", [P, 4], F32, s3)
        lt = sb("lt", [P, 4, NR], F32, s3)
        rt = {n: sb(f"rt_{n}", [P, 4, NEXP], F32, s3) for n in ("d", "e", "p", "is", "key", "oh1", "oh2", "p2", "oh")}
        rs4 = {n: sb(f"rs_{n}", [P, 4], F32, s3) for n in ("mx", "sum", "rec", "m1", "k1", "m2", "k2")}
        sg = sb("sg", [P, 4], F32, s3)
        cw = sb("cw", [P, 4, NR], F32, s3)
        cwr = sb("cwr", [P, 2, 4, NR], F32, s3)
        selb = sb("selb", [P, NIC * P], BF16, s3)
        combt = sb("combt", [P, 2, CH], BF16, s3)
        th = sb("th", [P, 2, CH], F32, s3)
        act_f = sb("act_f", [P, 2, CH], F32, s3)
        act_h = sb("act_h", [P, 2, CH], F32R, s3)
        act_l = sb("act_l", [P, 2, CH], F32R, s3)
        order = [(i - SLICE_OVER_A) % NIC for i in range(NIC)]
        mh, ml = [None] * NIC, [None] * NIC
        for ic in order:
            mh[ic] = sb(f"mh{ic}", [P, 6, P], F32R, s3)
            ml[ic] = sb(f"ml{ic}", [P, 6, P], F32R, s3)
        s3.close()

        p1 = ExitStack()
        tp = ps("tp", [P, CH], F32, p1)
        qt = ps("qt", [P, 4, P], F32, p1)
        pqk = [ps(f"pqk{i}", [P, CH], F32, p1) for i in range(2)]
        pva = [ps(f"pva{i}", [P, CH], F32, p1) for i in range(2)]
        pka = [ps(f"pka{i}", [P, CH], F32, p1) for i in range(2)]
        p1.close()
        p2 = ExitStack()
        mx = [ps(f"mx{i}", [P, CH], F32, p2) for i in range(3)]
        st = [ps(f"st{i}", [P, 2, CH], F32, p2) for i in range(2)]
        o = ps("o", [P, CH], F32, p2)
        p2.close()

        p3 = ExitStack()
        pg = [ps(f"pg{i}", [P, CH], F32, p3) for i in range(2)]
        pu = [ps(f"pu{i}", [P, CH], F32, p3) for i in range(2)]
        pc = ps("pc", [P, CH], F32, p3)
        py = [ps(f"py{i}", [P, CH], F32, p3) for i in range(2)]
        side = ps("side", [P, CH], F32, p3)
        p3.close()

        x_in = [sem(f"x_in{c}") for c in range(NCH)]
        w_in = [sem(f"w_in{n}") for n in range(3)]
        id_in = sem("id_in")
        c_in = sem("c_in")
        ln_in = sem("ln_in")
        bias_in = sem("bias_in")
        cst_bf = sem("cst_bf")
        half_set = sem("half_set")
        stats = sem("stats")
        rs_ln = sem("rs_ln")
        rs_rms = sem("rs_rms")
        rs_step = sem("rs_step")
        w_scaled = sem("w_scaled")
        w_hi = sem("w_hi")
        w_lo = sem("w_lo")
        xn_done = sem("xn_done")
        tp_ready = sem("tp_ready")
        x_hi = sem("x_hi")
        x_lo = sem("x_lo")
        mm_qk = sem("mm_qk")
        mm_va = sem("mm_va")
        mm_ka = sem("mm_ka")
        e_qk = sem("e_qk")
        e_v = sem("e_v")
        e_a = sem("e_a")
        biased = sem("biased")
        v_done = sem("v_done")
        rot_sin = sem("rot_sin")
        rot_cos = sem("rot_cos")
        roped = sem("roped")
        qt_ready = sem("qt_ready")
        q_hi = sem("q_hi")
        q_lo = sem("q_lo")
        sq_out = [sem(f"sq_out{i}") for i in range(2)]
        sa_out = [sem(f"sa_out{i}") for i in range(2)]
        sx_out = sem("sx_out")
        v_ones = sem("v_ones")
        q_zero = [sem(f"q_zero{i}") for i in range(2)]
        k_ones = [sem(f"k_ones{i}") for i in range(2)]
        stk_in = [sem(f"stk_in{i}") for i in range(2)]
        stk_first = sem("stk_first")
        zb_set = sem("zb_set")
        sz_out = sem("sz_out")
        mx_ready = sem("mx_ready")
        mx_read = sem("mx_read")
        nm_step = sem("nm_step")
        nm_ready = sem("nm_ready")
        nt_ready = sem("nt_ready")
        bn = sem("bn")
        nr_ready = sem("nr_ready")
        nr_out = [sem(f"nr_out{i}") for i in range(2)]
        nr_in = [sem(f"nr_in{i}") for i in range(4)]
        st_ready = sem("st_ready")
        exped = sem("exped")
        av_done = sem("av_done")
        o_zero = sem("o_zero")
        o_read = sem("o_read")
        ot_ready = sem("ot_ready")
        o_rec = sem("o_rec")
        ctx_ready = sem("ctx_ready")
        ctx_out = [sem(f"ctx_out{i}") for i in range(2)]
        a_in = [sem(f"a_in{i}") for i in range(2)]
        a_prod = sem("a_prod")
        a_log = sem("a_log")
        a_masked = sem("a_masked")
        a_max = sem("a_max")
        a_shift = sem("a_shift")
        a_exp = sem("a_exp")
        a_sum = sem("a_sum")
        a_rec = sem("a_rec")
        a_tree = sem("a_tree")
        a_done = sem("a_done")
        att_end = sem("att_end")
        ws_in = sem("ws_in")
        sel_in = sem("sel_in")
        comb_zero = sem("comb_zero")
        cb_zero = sem("cb_zero")
        half3_set = sem("half3_set")
        sel_zero = sem("sel_zero")
        m_in = [sem(f"m_in{i}") for i in range(2)]
        m_hi = sem("m_hi")
        m_lo = sem("m_lo")
        ws_hi = sem("ws_hi")
        ws_lo = sem("ws_lo")
        cx_in = sem("cx_in")
        xr_in = sem("xr_in")
        sd_ready = sem("sd_ready")
        sd_hi = sem("sd_hi")
        sd_read = sem("sd_read")
        x1_ready = sem("x1_ready")
        sq_done = sem("sq_done")
        ms_step = sem("ms_step")
        r2_ready = sem("r2_ready")
        res_x1 = sem("res_x1")
        hn_ready = sem("hn_ready")
        lt_done = sem("lt_done")
        rt_step = sem("rt_step")
        rt_exp = sem("rt_exp")
        cb_ready = sem("cb_ready")
        g_ready = sem("g_ready")
        u_ready = sem("u_ready")
        c_ready = sem("c_ready")
        th_ready = sem("th_ready")
        act_step = sem("act_step")
        ah_ready = sem("ah_ready")
        al_ready = sem("al_ready")
        y_used = sem("y_used")
        y_read = sem("y_read")
        out_ready = sem("out_ready")
        fin = sem("fin")

        def tiles(eng, step, before_last=None):
            for m in range(2):
                step(m, 0)
                step(m, 1)
            with eng.Fori(2, NT // 2 - 1) as m:
                step(m, 0)
                step(m, 1)
            if before_last:
                before_last()
            step(NT // 2 - 1, 0)
            step(NT // 2 - 1, 1)

        def tiles_of(c):
            return slice(4 * (NCH - 1 - c), 4 * (NCH - c))

        def at_least(tile, n):
            return not isinstance(tile, int) or tile >= n

        def at_most(tile, n):
            return not isinstance(tile, int) or tile <= n

        TREE_ALL = 4 + 13 + 1

        MAXIMA, EXPS, SUMS = 4, 5, 6
        A_STEPS = {0: 0, 1: 1, 2: 2, 3: 3, MAXIMA: 5, EXPS: 8, SUMS: 9}
        A_STEPS_PER_4 = 35
        a_steps = {}
        for t in range(NT):
            base = t * A_STEPS_PER_4 // 4
            for kind, step in A_STEPS.items():
                a_steps.setdefault(base + step, []).append((kind, t))

        OUTPUT = {1: "y_copy", 2: "out_a", 3: "out_b"}
        PREPARE = {4: ("turn_ctx0",), 5: ("turn_ctx1",), 6: ("proj_a",), 7: ("proj_b",), 8: ("normalise",), 9: ("turn_h0",),
                   10: ("turn_h1",), 11: ("logits",), 12: ("turn_logits", "softmax"), 13: ("largest",), 14: ("second",),
                   15: ("combine",), 16: ("turn_comb",)}
        PREP_ORDER = [w for k in sorted(PREPARE) for w in PREPARE[k]]

        def side_plan():
            plan = [(-1 if w == "turn_comb" else -2, w, 0) for w in PREP_ORDER]
            for c in range(NCH + 1):
                for ic in range(NIC):
                    if c >= 1 and ic in OUTPUT:
                        plan.append((c * NIC + ic, OUTPUT[ic], c - 1))
                    if c + 1 < NCH and ic in PREPARE:
                        plan += [(c * NIC + ic, w, c + 1) for w in PREPARE[ic]]
            return plan

        SIDE = side_plan()
        side_use = {(w, c): n for n, (w, c) in enumerate((w, c) for _, w, c in SIDE if w in BANKED)}
        M3 = NCH * NIC
        MS_AFTER = SLICES_AHEAD + 7

        def side_bank(w, c):
            return mx[BANK_AT["side", side_use[w, c]] % 3] if (w, c) in early_work else side

        early_work = {(w, 0) for w in EARLY_BANKED}

        def run_side(step, do):
            for at, w, c in SIDE:
                if at == step:
                    do(w, c)

        block = ctx.enter_context(nc.Block())

        @block.sync
        def _(sp):
            def load_x(c):
                sp.dma_start(res[:, 4 * c:4 * c + 4, :], xv[:, 4 * c:4 * c + 4, :]).then_inc(x_in[c], 16)

            def load_w(n):
                w = slice(n * CH, (n + 1) * CH)
                sp.dma_start(wraw[:, :, w], wproj.rearrange("(k p) n -> p k n", p=P)[:, :, w]).then_inc(w_in[n], 16)

            load_x(0)
            sp.dma_start(lnw[:, :, :], wln).then_inc(ln_in, 16)
            load_w(0)
            sp.dma_start(cst[:, 0:C_MMAX], consts[:, 0:C_MMAX]).then_inc(id_in, 16)
            load_w(1)
            load_w(2)
            sp.dma_start(bias[:, :], bqkv.partition_broadcast(P)).then_inc(bias_in, 16)
            sp.dma_start(cst[:, C_MMAX:C_ALL], consts[:, C_MMAX:C_ALL]).then_inc(c_in, 16)
            for c in range(1, NCH):
                load_x(c)

            def qk_out(m, par):
                sp.wait_ge(q_lo, 2 * m + par + 1)
                for piece, src in ((0, sth), (1, stl)):
                    sp.dma_start(sq[piece].rearrange("(c p) n -> p c n", p=P)[:, :, bass.ds((2 * m + par) * P, P)],
                                 src[:, par, :, :].bitcast(F32)).then_inc(sq_out[par], 16)

            def step(m, par):
                t = 2 * m + par
                if at_least(t, 1):
                    if par:
                        qk_out(m, 0)
                    else:
                        qk_out(m - 1, 1)
                sp.wait_ge(e_a, t + 1)
                sp.dma_start(sa[bass.ds(t, 1), :, :].rearrange("a p n -> p (a n)"), asb[:, par, :]).then_inc(sa_out[par], 16)
                sp.wait_ge(xn_done, t + 1)
                sp.dma_start(sx[:, bass.ds(t, 1), :], xn[:, bass.ds(t, 1), :]).then_inc(sx_out, 16)

            def load_stack(g, cols, landed):
                for dst, base, order in ((qs, 0, (0, 0, 1)), (ks, D, (0, 1, 0))):
                    for b, piece in enumerate(order):
                        src = sq[piece][base + 64 * g:base + 64 * g + 64, cols].rearrange("(s e d) n -> e d s n", s=2, e=2)
                        for e in range(2):
                            rows = slice(KROWS * e + HD * b, KROWS * e + HD * b + HD)
                            into = qs[g % 2][rows, :, e, cols] if dst is qs else ks[g % 2][rows, :, cols]
                            sp.dma_start(into.bitcast(F32), src[e]).then_inc(landed, 16)
                if g >= 2:
                    sp.wait_ge(sz_out, 16)
                    sp.dma_start(qs[g % 2][2 * KROWS:2 * KROWS + 2, :, :, :].bitcast(F32), sz).then_inc(landed, 16)

            def early():
                sp.wait_ge(zb_set, 1)
                sp.dma_start(sz.rearrange("a b c (x n) -> (a b c x) n", n=CH // 2), zb[0:8 * T * 2 // CH, :].bitcast(F32)).then_inc(sz_out, 16)
                sp.wait_ge(sq_out[0], 32 * (NT // 2 - 1))
                sp.wait_ge(sq_out[1], 32 * (NT // 2 - 2))
                sp.wait_ge(k_ones[0], 1)
                sp.wait_ge(q_zero[0], 1)
                load_stack(0, slice(0, FIRST_COLS), stk_first)

            tiles(sp, step, early)
            qk_out(NT // 2 - 1, 1)
            for par in range(2):
                sp.wait_ge(sq_out[par], 32 * (NT // 2))
            load_stack(0, slice(FIRST_COLS, T), stk_in[0])
            for par in range(2):
                sp.wait_ge(sa_out[par], 16 * (NT // 2))

            def load_a(t):
                if t >= 2:
                    sp.wait_ge(a_done, t - 1)
                sp.dma_start(ain[:, t % 2, :], sa[t]).then_inc(a_in[t % 2], 16)

            sp.wait_ge(sx_out, 16 * NT)
            sp.wait_ge(v_done, NT)
            sp.wait_ge(mm_ka, NT)
            load_a(0)
            load_a(1)
            next_a = 2
            sp.wait_ge(k_ones[1], 1)
            load_stack(1, slice(0, T), stk_in[1])

            def load_chunk(c):
                sp.dma_start(ctxin[:, :, :], sc[:, tiles_of(c), :]).then_inc(cx_in, 16)
                sp.dma_start(xin[:, :, :], sx[:, tiles_of(c), :]).then_inc(xr_in, 16)

            def load_slice(ic):
                sp.dma_start(mraw[:, ic % 2, :, :], wmoe[ic].rearrange("p (a n) -> p a n", a=6)).then_inc(m_in[ic % 2], 16)

            for s in range(-1, NS + 3):
                for kind, u in TURNS.get(s - 1, []) if s > -1 else []:
                    g, c = UNITS[u]
                    if kind == "neg":
                        sp.wait_ge(nr_ready, u + 1)
                        sp.dma_start(sn[u], nmr[:, u % 2, :]).then_inc(nr_out[u % 2], 16)
                        sp.wait_ge(nr_out[u % 2], 16 * (u // 2 + 1))
                        for e in range(2):
                            sp.dma_start(qs[g % 2][2 * KROWS:2 * KROWS + 2, :, e, c * CH:(c + 1) * CH].bitcast(F32),
                                         sn[u, 4 * e:4 * e + 4, :].rearrange("(a b) n -> a b n", a=2)).then_inc(nr_in[u % 4], 16)
                for u in range(NU):
                    if s == UNIT_LAST[u] + 3:
                        g, c = UNITS[u]
                        sp.wait_ge(ctx_ready, u + 1)
                        sp.dma_start(sc[:, 4 * c:4 * c + 4, 64 * g:64 * g + 64], ctxs[:, u % 2, :, :]).then_inc(ctx_out[u % 2], 16)
                        if u % NCH == NCH - 1 and g + 2 < NG:
                            sp.wait_ge(av_done, UNIT_LAST[u] + 1)
                            load_stack(g + 2, slice(0, T), stk_in[g % 2])
                if s == EARLY_AT - 3:
                    sp.wait_ge(av_done, STACKS_FREE)
                    sp.dma_start(woraw[:, :, :], wo.rearrange("(k p) n -> p k n", p=P)).then_inc(ws_in, 16)
                    sp.dma_start(wrraw[:, :, :], wr.rearrange("(k p) n -> p k n", p=P)).then_inc(ws_in, 16)
                    for i in range(2):
                        sp.wait_ge(ctx_out[i], 16 * sum(u % 2 == i for u in range(NU - NCH + 1)))
                    load_chunk(0)
                    load_slice(0)
                    load_slice(1)
                if s == NS - 4:
                    sp.wait_ge(m_lo, 1)
                    load_slice(2)
                if next_a < NT and s == (next_a - 1) * A_STEPS_PER_4 // 4:
                    load_a(next_a)
                    next_a += 1

            sp.wait_ge(att_end, 4)
            for i in range(2):
                sp.wait_ge(ctx_out[i], 16 * NU // 2)
            for i in range(4):
                sp.wait_ge(nr_in[i], 32 * NU // 4)

            def load_next(c):
                sp.wait_ge(sd_read, side_use["turn_h1", c - 1] + 1)
                load_chunk(c)

            load_next(1)
            for ic in range(3, NIC):
                sp.wait_ge(m_lo, ic - 1)
                load_slice(ic)
            for c in range(1, NCH + 1):
                if 2 <= c < NCH:
                    load_next(c)
                for n in range(2):
                    sp.wait_ge(out_ready, 2 * (c - 1) + n + 1)
                    t2 = slice(tiles_of(c - 1).start + 2 * n, tiles_of(c - 1).start + 2 * n + 2)
                    sp.dma_start(outv[:, t2, :], res[:, t2, :]).then_inc(fin, 16)
            sp.wait_ge(fin, 16 * 2 * NCH)

        @block.gpsimd
        def _(pool):
            pool.memset(half[:, :], -0.5).then_inc(half_set, 1)
            pool.memset(qs[0][:, :, :, :].bitcast(F32), 0.0).then_inc(q_zero[0], 1)

            def factors(c):
                t4 = slice(4 * c, 4 * c + 4)
                pool.wait_ge(stats, c + 1)
                pool.tensor_scalar(tmpr[:, t4], mv[:, t4, 1], LN_EPS, None, ALU.add).then_inc(rs_step, 1)
                pool.wait_ge(rs_step, 4 * c + 1)
                pool.tensor_tensor(rstd[:, t4], tmpr[:, t4], half[:, :], ALU.pow).then_inc(rs_ln, 4)
                pool.wait_ge(rs_ln, 4 * c + 4)
                pool.tensor_tensor(tmpr[:, t4], rstd[:, t4], rstd[:, t4], ALU.mult).then_inc(rs_step, 1)
                pool.wait_ge(rs_step, 4 * c + 2)
                pool.tensor_tensor(tmpr[:, t4], tmpr[:, t4], mv[:, t4, 1], ALU.mult).then_inc(rs_step, 1)
                pool.wait_ge(rs_step, 4 * c + 3)
                pool.tensor_scalar(tmpr[:, t4], tmpr[:, t4], RMS_EPS, None, ALU.add).then_inc(rs_step, 1)
                pool.wait_ge(rs_step, 4 * c + 4)
                pool.tensor_tensor(rms1[:, t4], tmpr[:, t4], half[:, :], ALU.pow).then_inc(rs_rms, 4)

            pool.wait_ge(half_set, 1)
            factors(0)
            pool.memset(v[:, :, :, HD:VC], 1.0).then_inc(v_ones, 1)
            pool.wait_ge(bias_in, 16)
            pool.wait_ge(c_in, 16)

            def step(m, par):
                t = 2 * m + par
                pool.wait_ge(e_qk, t + 1)
                pool.tensor_tensor(qksb[:, par, :], qksb[:, par, :], bias[:, 0:2 * D], ALU.add).then_inc(biased, 1)
                pool.wait_ge(e_v, t + 1)
                pool.tensor_tensor(v[:, bass.ds(t, 1), :, 0:HD].rearrange("p a h d -> p (a h) d"),
                                   vst[:, par, :].rearrange("p (h d) -> p h d", h=H),
                                   bias[:, 2 * D:3 * D].rearrange("p (h d) -> p h d", h=H), ALU.add).then_inc(v_done, 1)
                pool.wait_ge(biased, t + 1)
                if at_least(t, 2):
                    pool.wait_ge(roped, t - 1)
                src = qksb[:, par, :].rearrange("p (q h f e) -> p q h f e", q=2, h=H, f=2)
                dst = rt2[:, par, :].rearrange("p (q h f e) -> p q h f e", q=2, h=H, f=2)
                sn_t = cst[:, bass.ds(C_SIN + t * 32, 32)].rearrange("p (q f e) -> p q f e", q=2, f=2)
                for f in range(2):
                    last = pool.tensor_tensor(dst[:, :, :, f, :], src[:, :, :, 1 - f, :],
                                              sn_t[:, :, f, :].unsqueeze(2).broadcast_to([P, 2, H, 8]), ALU.mult)
                last.then_inc(rot_sin, 1)
                if isinstance(t, int) and t + 1 < NCH:
                    factors(t + 1)

            tiles(pool, step)
            pool.wait_ge(roped, NT)
            pool.wait_ge(q_lo, NT)
            pool.wait_ge(mm_ka, NT)
            pool.wait_ge(sx_out, 16 * NT)
            for i in range(2):
                pool.wait_ge(sa_out[i], 16 * (NT // 2))
                pool.wait_ge(sq_out[i], 32 * (NT // 2))

            pool.memset(qs[1][:, :, :, :].bitcast(F32), 0.0).then_inc(q_zero[1], 1)
            pool.wait_ge(q_zero[1], 1)
            pool.memset(ks[1][96:128, :, :].bitcast(F32), 1.0).then_inc(k_ones[1], 1)
            pool.wait_ge(k_ones[1], 1)

            def products(t, m, par):
                pool.wait_ge(a_in[par], 16 * (m + 1))
                if at_least(t, 1):
                    pool.wait_ge(a_log, t)
                for b in range(4):
                    n = 4 * (b + 1)
                    q = ain[:, par, 4 * b * HD:4 * (b + 1) * HD].rearrange("p (h d) -> p h d", d=HD)
                    k = ain[:, par, D:D + n * HD].rearrange("p (g d) -> p g d", d=HD)
                    last = pool.tensor_tensor(qkp[b][:, :, :, :], q.unsqueeze(2).broadcast_to([P, 4, n, HD]),
                                              k.unsqueeze(1).broadcast_to([P, 4, n, HD]), ALU.mult)
                last.then_inc(a_prod, 1)

            def token_tile(m, par, last_tile=False):
                t = 2 * m + par
                pool.wait_ge(a_log, t + 1)
                pool.tensor_tensor(amask[:, :, :], alog[:, :, :], mask_a, ALU.add).then_inc(a_masked, 1)
                if not last_tile:
                    products(t + 1, m + par, 1 - par)
                pool.wait_ge(a_max, t + 1)
                pool.tensor_tensor(ashift[:, :, :], amask[:, :, :], amx[:, :].unsqueeze(2).broadcast_to([P, H, H]),
                                   ALU.subtract).then_inc(a_shift, 1)
                pool.wait_ge(a_exp, t + 1)
                if at_least(t, 1):
                    pool.wait_ge(a_done, t)
                for b in range(4):
                    n = 4 * (b + 1)
                    vv = ain[:, par, 2 * D:2 * D + n * HD].rearrange("p (g d) -> p g d", d=HD)
                    pool.tensor_tensor(avp[b][:, :, :, :], aexp[:, 4 * b:4 * b + 4, 0:n].unsqueeze(3).broadcast_to([P, 4, n, HD]),
                                       vv.unsqueeze(1).broadcast_to([P, 4, n, HD]), ALU.mult).then_inc(a_tree, 1)
                left = {b: 4 * (b + 1) for b in range(4)}
                pending = {b: b + 1 for b in range(4)}
                issued = 4
                while left:
                    for b in sorted(left):
                        n = left[b]
                        pool.wait_ge(a_tree, t * TREE_ALL + pending[b])
                        if n == 2:
                            dst, lo, hi = aout[:, 4 * b:4 * b + 4, :], avp[b][:, :, 0, :], avp[b][:, :, 1, :]
                        elif n == 3:
                            dst, lo, hi = avp[b][:, :, 0, :], avp[b][:, :, 0, :], avp[b][:, :, 2, :]
                        else:
                            dst, lo, hi = (avp[b][:, :, 0:n // 2, :].rearrange("p h g d -> p h (g d)"),
                                           avp[b][:, :, 0:n // 2, :].rearrange("p h g d -> p h (g d)"),
                                           avp[b][:, :, n // 2:n, :].rearrange("p h g d -> p h (g d)"))
                        pool.tensor_tensor(dst, lo, hi, ALU.add).then_inc(a_tree, 1)
                        issued += 1
                        pending[b] = issued
                        if n == 2:
                            del left[b]
                        else:
                            left[b] = 2 if n == 3 else n // 2
                assert issued + 1 == TREE_ALL
                pool.wait_ge(a_rec, t + 1)
                pool.wait_ge(a_tree, t * TREE_ALL + issued)
                pool.tensor_tensor(ascl[:, :, :], aout[:, :, :], arec[:, :].unsqueeze(2).broadcast_to([P, H, HD]),
                                   ALU.mult).then_inc(a_tree, 1)
                pool.wait_ge(a_tree, t * TREE_ALL + issued + 1)
                rt = res[:, bass.ds(t, 1), :].rearrange("p a d -> p (a d)")
                pool.tensor_tensor(rt, rt, ascl[:, :, :].rearrange("p h d -> p (h d)"), ALU.add).then_inc(a_done, 1)

            products(0, 0, 0)
            token_tile(0, 0)
            token_tile(0, 1)
            with pool.Fori(1, NT // 2 - 1) as m:
                token_tile(m, 0)
                token_tile(m, 1)
            token_tile(NT // 2 - 1, 0)
            token_tile(NT // 2 - 1, 1, last_tile=True)


            pool.wait_ge(a_done, NT)
            pool.wait_ge(av_done, STACKS_FREE)
            pool.memset(half3[:, :], -0.5).then_inc(half3_set, 1)
            pool.wait_ge(half3_set, 1)

            def mean_squares(c):
                pool.wait_ge(sq_done, c + 1)
                pool.tensor_scalar(msq1[:, :], msq[:, :], 1.0 / D, RMS_EPS, ALU.mult, ALU.add).then_inc(ms_step, 1)
                pool.wait_ge(ms_step, c + 1)
                pool.tensor_tensor(rms2[:, :], msq1[:, :], half3[:, :], ALU.pow).then_inc(r2_ready, 1)
                rt4 = res[:, tiles_of(c), :]
                pool.tensor_tensor(rt4, rt4, x1[:, :, :], ALU.add).then_inc(res_x1, 1)

            def lo_of_slice(ic):
                pool.wait_ge(m_hi, ic + 1)
                pool.tensor_tensor(ml[ic][:, :, :], mraw[:, ic % 2, :, :], mh[ic][:, :, :].bitcast(F32),
                                   ALU.subtract).then_inc(m_lo, 1)

            mean_squares(0)
            for ic in range(SLICES_AHEAD):
                lo_of_slice(ic)

            pool.sem_inc(att_end, 1)
            pool.wait_ge(att_end, 4)
            pool.memset(selb[:, :], 0.0).then_inc(sel_zero, 1)
            pool.wait_ge(sel_zero, 1)
            pool.dma_start(selb[0:3 * NR, :], sel).then_inc(sel_in, 16)
            for ic in range(SLICES_AHEAD, NIC):
                lo_of_slice(ic)
                if ic == MS_AFTER:
                    mean_squares(1)
            for c in range(2, NCH):
                mean_squares(c)

        @block.scalar
        def _(act):
            def hi_of_w(n):
                if n < 2:
                    act.wait_ge(w_scaled, n + 1)
                else:
                    act.wait_ge(w_in[n], 16)
                act.activation(wh[:, :, n * CH:(n + 1) * CH], wraw[:, :, n * CH:(n + 1) * CH], ACT.Copy).then_inc(w_hi, 1)

            hi_of_w(0)

            def hi_of_x(t, par):
                act.wait_ge(tp_ready, t + 1)
                if at_least(t, 2):
                    act.wait_ge(mm_ka, t - 1)
                act.activation(xh[:, par, :, :], tp[:, 0:KC * P].rearrange("p (k n) -> p k n", k=KC), ACT.Copy).then_inc(x_hi, 1)

            def hi_of_q(m, par):
                t = 2 * m + par
                act.wait_ge(qt_ready, t + 1)
                if at_least(m, 1):
                    act.wait_ge(sq_out[par], 32 * m)
                act.activation(sth[:, par, :, :], qt[:, :, :], ACT.Copy).then_inc(q_hi, 1)

            hi_of_x(0, 0)
            hi_of_w(1)
            hi_of_w(2)
            act.wait_ge(rs_rms, 4)

            def step(m, par):
                t = 2 * m + par
                if at_most(t, NT - 2):
                    hi_of_x(t + 1, 1 - par)
                scale = rms1[:, bass.ds(t, 1)]
                act.wait_ge(rs_rms, t + 1)
                act.wait_ge(mm_qk, t + 1)
                if at_least(t, 2):
                    act.wait_ge(roped, t - 1)
                act.activation(qksb[:, par, :], pqk[par][:, :], ACT.Copy, scale=scale).then_inc(e_qk, 1)
                act.wait_ge(mm_va, t + 1)
                if at_least(t, 2):
                    act.wait_ge(v_done, t - 1)
                if at_least(m, 1):
                    act.wait_ge(sa_out[par], 16 * m)
                act.activation(asb[:, par, 0:D], pva[par][:, D:2 * D], ACT.Copy)
                act.activation(vst[:, par, :], pva[par][:, 0:D], ACT.Copy, scale=scale).then_inc(e_v, 1)
                act.wait_ge(mm_ka, t + 1)
                act.activation(asb[:, par, D:3 * D], pka[par][:, :], ACT.Copy).then_inc(e_a, 1)
                if at_least(t, 1):
                    if par:
                        hi_of_q(m, 0)
                    else:
                        hi_of_q(m - 1, 1)

            tiles(act, step)
            hi_of_q(NT // 2 - 1, 1)
            act.wait_ge(q_lo, NT)
            act.wait_ge(v_done, NT)
            act.wait_ge(sx_out, 16 * NT)
            for i in range(2):
                act.wait_ge(sa_out[i], 16 * (NT // 2))
                act.wait_ge(sq_out[i], 32 * (NT // 2))

            def side_act(w, c):
                bank = side_bank(w, c)
                if w in BANKED:
                    ready = side_use[w, c] + 1
                if w in ("turn_ctx0", "turn_ctx1"):
                    act.wait_ge(sd_ready, ready)
                    act.activation(cth[:, int(w[-1]), :], bank[:, :], ACT.Copy).then_inc(sd_hi, 1)
                elif w in ("turn_h0", "turn_h1"):
                    k = int(w[-1])
                    act.wait_ge(sd_ready, ready)
                    act.activation(hth[:, c % 2, k, :], bank[:, :], ACT.Copy, scale=lnw[:, 1, k:k + 1]).then_inc(sd_hi, 1)
                elif w == "logits":
                    act.wait_ge(sd_ready, ready)
                    act.activation(lg[:, :], bank[0:NR, :], ACT.Copy).then_inc(sd_read, 1)
                elif w == "softmax":
                    act.wait_ge(lt_done, c + 1)
                    act.activation(rt["e"][:, :, :], rt["d"][:, :, :], ACT.Exp)
                    act.activation(sg[:, :], lt[:, :, NEXP], ACT.Tanh, scale=0.5).then_inc(rt_exp, 1)
                elif w == "turn_comb":
                    act.wait_ge(sd_ready, ready)
                    act.wait_ge(comb_zero, 1)
                    act.activation(combt[0:32, c % 2, :], bank[:, :].bitcast(BF16)[0:32, 0:CH], ACT.Copy).then_inc(sd_read, 1)
                elif w == "y_copy":
                    act.wait_ge(y_used, NIC * (c + 1))
                    act.wait_ge(res_x1, min(c + 2, NCH))
                    act.wait_ge(hn_ready, min(c + 2, NCH))
                    for f in range(2):
                        last = act.activation(x1[:, 2 * f:2 * f + 2, :].rearrange("p a n -> p (a n)"), py[f][:, :], ACT.Copy)
                    last.then_inc(y_read, 1)

            def split_weights(ic):
                act.wait_ge(m_in[ic % 2], 16 * (ic // 2 + 1))
                act.activation(mh[ic][:, :, :], mraw[:, ic % 2, :, :], ACT.Copy).then_inc(m_hi, 1)

            def exp_pair(s, pr):
                off = first_key_column(s)
                act.wait_ge(st_ready, 2 * s + pr + 1)
                if s >= 2:
                    act.wait_ge(av_done, s - 1)
                act.activation(pt[:, s % 2, pr, :, off:CH], st[pr][:, :, off:CH], ACT.Exp).then_inc(exped, 1)

            def neg_rows(u):
                act.wait_ge(nt_ready, u + 1)
                if u >= 2:
                    act.wait_ge(nr_out[u % 2], 16 * (u // 2))
                act.activation(nmr[:, u % 2, :], mx[BANK_AT["neg", u] % 3][0:8, :], ACT.Copy).then_inc(nr_ready, 1)

            for s in range(-1, NS + 3):
                if 0 <= s < NS:
                    exp_pair(s, 0)
                if s - 1 in UNIT_LAST:
                    u = UNIT_LAST.index(s - 1)
                    act.wait_ge(av_done, s)
                    if u >= 1:
                        act.wait_ge(ot_ready, u)
                    act.activation(osb[:, :], o[:, :], ACT.Copy).then_inc(o_read, 1)
                if 0 <= s < NS:
                    exp_pair(s, 1)
                if s - 1 in EARLY:
                    side_act(EARLY[s - 1], 0)
                if s in SPLIT_AT:
                    act.wait_ge(a_done, NT)
                    split_weights(SPLIT_AT.index(s))
                if s == EARLY_AT - 1:
                    act.wait_ge(ws_in, 32)
                    act.activation(woh[:, :, :], woraw[:, :, :], ACT.Copy).then_inc(ws_hi, 1)
                    act.activation(wrh[:, :, :], wrraw[:, :, :], ACT.Copy).then_inc(ws_hi, 1)
                for kind, u in TURNS.get(s, []):
                    if kind == "neg":
                        neg_rows(u)
                for kind, t in a_steps.get(s, []):
                    if kind == EXPS:
                        act.wait_ge(a_shift, t + 1)
                        if t >= 1:
                            act.wait_ge(a_tree, TREE_ALL * (t - 1) + 4)
                        act.activation(aexp[:, :, :], ashift[:, :, :], ACT.Exp).then_inc(a_exp, 1)


            act.wait_ge(o_read, NU)
            act.sem_inc(att_end, 1)
            act.wait_ge(att_end, 4)

            run_side(-1, side_act)
            ahead = SLICES_AHEAD
            for n in range(M3 + 4):
                if n < M3:
                    act.wait_ge(g_ready, n + 1)
                    if n >= 2:
                        act.wait_ge(act_step, 3 * (n - 2) + 1)
                    act.activation(th[:, n % 2, :], pg[n % 2][:, :], ACT.Tanh, scale=0.5).then_inc(th_ready, 1)
                    if ahead < NIC:
                        split_weights(ahead)
                        ahead += 1
                    if n % NIC == 1 and n > NIC:
                        side_act("y_copy", n // NIC - 1)
                    act.wait_ge(act_step, 3 * n + 3)
                    if n >= 2:
                        act.wait_ge(y_used, n - 1)
                    act.activation(act_h[:, n % 2, :], act_f[:, n % 2, :], ACT.Copy).then_inc(ah_ready, 1)
                for at, w, c in SIDE:
                    if at == n and (w != "y_copy" or n >= M3):
                        side_act(w, c)

        @block.vector
        def _(dve):
            dve.memset(zb[:, :], 0.0).then_inc(zb_set, 1)
            dve.memset(ks[0][96:128, :, :].bitcast(F32), 1.0).then_inc(k_ones[0], 1)
            def statistics(c):
                dve.wait_ge(x_in[c], 16)
                for t in range(4 * c, 4 * c + 4):
                    last = dve.bn_stats(bst[:, t, :], res[:, t, :])
                last.then_inc(bn, 1)
                dve.wait_ge(bn, c + 1)
                for t in range(4 * c, 4 * c + 4):
                    last = dve.bn_aggr(mv[:, t, :], bst[:, t, :])
                last.then_inc(stats, 1)

            def scale_w(n, cols):
                dve.wait_ge(w_in[n], 16)
                for k in range(KC):
                    last = dve.tensor_scalar(wraw[:, k, cols], wraw[:, k, cols], lnw[:, 0, k:k + 1], None, ALU.mult)
                last.then_inc(w_scaled, 1)

            def lo_of_w(n):
                dve.wait_ge(w_hi, n + 1)
                w = slice(n * CH, (n + 1) * CH)
                dve.tensor_tensor(wl[:, :, w], wraw[:, :, w], wh[:, :, w].bitcast(F32), ALU.subtract).then_inc(w_lo, 1)

            def normalise(t, par):
                dve.wait_ge(rs_ln, t + 1)
                if at_least(t, 2):
                    dve.wait_ge(tp_ready, t - 1)
                for dst in (xnp[:, par, :], xn[:, bass.ds(t, 1), :].rearrange("p a d -> p (a d)")):
                    last = dve.tensor_scalar(dst, res[:, bass.ds(t, 1), :].rearrange("p a d -> p (a d)"),
                                             mv[:, bass.ds(t, 1), 0], rstd[:, bass.ds(t, 1)], ALU.subtract, ALU.mult)
                last.then_inc(xn_done, 1)

            def lo_of_x(t, par):
                dve.wait_ge(x_hi, t + 1)
                if at_least(t, 2):
                    dve.wait_ge(mm_ka, t - 1)
                dve.tensor_tensor(xl[:, par, :, :], tp[:, 0:KC * P].rearrange("p (k n) -> p k n", k=KC),
                                  xh[:, par, :, :].bitcast(F32), ALU.subtract).then_inc(x_lo, 1)

            def lo_of_q(m, par):
                t = 2 * m + par
                dve.wait_ge(q_hi, t + 1)
                dve.tensor_tensor(stl[:, par, :, :], qt[:, :, :], sth[:, par, :, :].bitcast(F32), ALU.subtract).then_inc(q_lo, 1)

            statistics(0)
            dve.wait_ge(ln_in, 16)
            scale_w(0, slice(0, CH))
            normalise(0, 0)
            lo_of_w(0)
            lo_of_x(0, 0)
            scale_w(1, slice(CH, CH + D))
            normalise(1, 1)
            lo_of_w(1)
            lo_of_w(2)

            def step(m, par):
                t = 2 * m + par
                if at_most(t, NT - 3):
                    normalise(t + 2, par)
                if at_most(t, NT - 2):
                    lo_of_x(t + 1, 1 - par)
                if isinstance(t, int) and t + 1 < NCH:
                    statistics(t + 1)
                if isinstance(t, int) and t == 0:
                    dve.wait_ge(c_in, 16)
                    dve.wait_ge(id_in, 16)
                    dve.tensor_copy(identb[:, :], ident)
                    dve.tensor_copy(mmaxb[:, :], cst[:, C_MMAX:C_MMAX + P])
                    dve.tensor_copy(mstb[:, :], cst[:, C_MST:C_MST + P]).then_inc(cst_bf, 1)
                dve.wait_ge(biased, t + 1)
                cs_t = cst[:, bass.ds(C_COS + t * 16, 16)].rearrange("p (q e) -> p q e", q=2)
                if at_least(t, 2):
                    dve.wait_ge(roped, t - 1)
                dve.tensor_tensor(rt1[:, par, :].rearrange("p (q f e) -> p q f e", q=2, e=8),
                                  qksb[:, par, :].rearrange("p (q f e) -> p q f e", q=2, e=8),
                                  cs_t.unsqueeze(2).broadcast_to([P, 2, 2 * H, 8]), ALU.mult).then_inc(rot_cos, 1)
                dve.wait_ge(rot_cos, t + 1)
                dve.wait_ge(rot_sin, t + 1)
                if at_least(t, 2):
                    dve.wait_ge(qt_ready, t - 1)
                dve.tensor_tensor(qkr[:, par, :], rt1[:, par, :], rt2[:, par, :], ALU.add).then_inc(roped, 1)
                if at_least(t, 1):
                    if par:
                        lo_of_q(m, 0)
                    else:
                        lo_of_q(m - 1, 1)

            tiles(dve, step)
            lo_of_q(NT // 2 - 1, 1)


            def take_max(i):
                u, r, pairs, e, k0, w, _ = PIECES[i]
                dve.wait_ge(mx_ready, i + 1)
                if u >= 2:
                    dve.wait_ge(nm_step, 2 * (u - 2) + 1)
                dve.tensor_reduce(mxp[:, u % 2, r, pairs[0]:pairs[-1] + 1, e, k0 // CH],
                                  mx[BANK_AT["piece", i] % 3][:, 0:w * len(pairs)].rearrange("p (s k) -> p s k", k=w),
                                  AX.X, ALU.max).then_inc(mx_read, 1)

            def negate(u):
                c = UNITS[u][1]
                dve.wait_ge(mx_read, PIECE_END[u])
                if u >= 1:
                    dve.wait_ge(nm_ready, u)
                dve.tensor_reduce(nmx[:, :, :, :], mxp[:, u % 2, :, :, :, 0:c + 1], AX.X, ALU.max, negate=True).then_inc(nm_step, 1)
                dve.wait_ge(nm_step, 2 * u + 1)
                if u >= 2:
                    dve.wait_ge(nt_ready, u - 1)
                dst = nmt[:, u % 2, :, :].rearrange("p r (e a s) -> p r e a s", e=2, a=2)
                src = nmx[:, :, :, :].rearrange("p r s e -> p r e s")
                dve.tensor_copy(dst[:, :, :, 0, :], src).then_inc(nm_step, 1)
                dve.wait_ge(nm_step, 2 * u + 2)
                dve.tensor_tensor(dst[:, :, :, 1, :], src, dst[:, :, :, 0, :].bitcast(F32), ALU.subtract).then_inc(nm_ready, 1)

            def context(u):
                dve.wait_ge(ot_ready, u + 1)
                if u >= 1:
                    dve.wait_ge(ctx_ready, u)
                ov = mx[BANK_AT["ctx", u] % 3][:, :].rearrange("p (r j d) -> p r j d", r=CH // P, j=G)
                dve.reciprocal(orec[:, :, :], ov[:, :, :, HD]).then_inc(o_rec, 1)
                dve.wait_ge(o_rec, u + 1)
                if u >= 2:
                    dve.wait_ge(ctx_out[u % 2], 16 * (u // 2))
                dve.tensor_tensor(ctxs[:, u % 2, :, :].rearrange("p r (j d) -> p r j d", j=G), ov[:, :, :, 0:HD],
                                  orec[:, :, :].unsqueeze(3).broadcast_to([P, CH // P, G, HD]),
                                  ALU.mult).then_inc(ctx_ready, 1)

            def over_heads(kind, t):
                if kind < 4:
                    if kind == 0:
                        dve.wait_ge(a_prod, t + 1)
                        if t >= 1:
                            dve.wait_ge(a_masked, t)
                        else:
                            dve.wait_ge(a_sum, 1)
                    ins = dve.tensor_reduce(alog[:, 4 * kind:4 * kind + 4, 0:4 * (kind + 1)], qkp[kind][:, :, :, :], AX.X, ALU.add)
                    if kind == 3:
                        ins.then_inc(a_log, 1)
                elif kind == MAXIMA:
                    dve.wait_ge(a_masked, t + 1)
                    dve.tensor_reduce(amx[:, :], amask[:, :, :], AX.X, ALU.max).then_inc(a_max, 1)
                elif kind == SUMS:
                    dve.wait_ge(a_exp, t + 1)
                    if t >= 1:
                        dve.wait_ge(a_rec, t)
                    dve.tensor_reduce(asum[:, :], aexp[:, :, :], AX.X, ALU.add).then_inc(a_sum, 1)
                    dve.wait_ge(a_sum, t + 2)
                    if t >= 1:
                        dve.wait_ge(a_done, t)
                    dve.reciprocal(arec[:, :], asum[:, :]).then_inc(a_rec, 1)

            steps = [0]

            def small(ins):
                ins.then_inc(rt_step, 1)
                steps[0] += 1
                dve.wait_ge(rt_step, steps[0])

            def wide(a):
                return a[:, :].unsqueeze(2).broadcast_to([P, 4, NEXP])

            def pick(src, m, k, onehot):
                key = cst[:, C_KEY:C_KEY + NEXP].unsqueeze(1).broadcast_to([P, 4, NEXP])
                small(dve.tensor_reduce(rs4[m][:, :], rt[src][:, :, :], AX.X, ALU.max))
                small(dve.tensor_tensor(rt["is"][:, :, :], rt[src][:, :, :], wide(rs4[m]), ALU.is_equal))
                small(dve.tensor_tensor(rt["key"][:, :, :], rt["is"][:, :, :], key, ALU.mult))
                small(dve.tensor_reduce(rs4[k][:, :], rt["key"][:, :, :], AX.X, ALU.max))
                small(dve.tensor_tensor(rt[onehot][:, :, :], rt["key"][:, :, :], wide(rs4[k]), ALU.is_equal))

            def side_dve(w, c):
                bank = side_bank(w, c)
                if w in BANKED:
                    use = side_use[w, c]
                if w in ("turn_ctx0", "turn_ctx1"):
                    k = int(w[-1])
                    dve.wait_ge(sd_hi, 4 * c + k + 1)
                    dve.tensor_tensor(ctl[:, k, :], bank[:, :], cth[:, k, :].bitcast(F32), ALU.subtract).then_inc(sd_read, 1)
                elif w in ("proj_a", "proj_b"):
                    r = slice(0, 2) if w == "proj_a" else slice(2, 4)
                    dve.wait_ge(sd_ready, use + 1)
                    dve.wait_ge(xr_in, 16 * (c + 1))
                    if c >= 1:
                        dve.wait_ge(res_x1, c)
                    if c >= 2:
                        dve.wait_ge(sd_ready, side_use["out_b", c - 2] + 1)
                    dve.tensor_tensor(x1[:, r, :], bank[:, :].rearrange("p (r n) -> p r n", r=2), xin[:, r, :],
                                      ALU.add).then_inc(sd_read, 1)
                    if w == "proj_b":
                        dve.wait_ge(sd_read, use + 1)
                        if c >= 1:
                            dve.wait_ge(r2_ready, c)
                        for i in range(4):
                            if c or i:
                                dve.wait_ge(x1_ready, 4 * c + i)
                            dve.tensor_tensor_reduce(sqj[:, :], x1[:, i, :], x1[:, i, :], 1.0, 0.0, ALU.mult, ALU.add,
                                                     msq[:, i:i + 1]).then_inc(x1_ready, 1)
                        dve.wait_ge(x1_ready, 4 * c + 4)
                        dve.sem_inc(sq_done, 1)
                elif w == "normalise":
                    dve.wait_ge(r2_ready, c + 1)
                    for i in range(4):
                        last = dve.tensor_scalar(ctxin[:, i, :], x1[:, i, :], rms2[:, i:i + 1], None, ALU.mult)
                    last.then_inc(hn_ready, 1)
                elif w in ("turn_h0", "turn_h1"):
                    k = int(w[-1])
                    dve.wait_ge(sd_hi, 4 * c + 2 + k + 1)
                    dve.scalar_tensor_tensor(out=htl[:, c % 2, k, :], in0=bank[:, :], scalar=lnw[:, 1, k:k + 1],
                                             in1=hth[:, c % 2, k, :].bitcast(F32), op0=ALU.mult, op1=ALU.subtract).then_inc(sd_read, 1)
                elif w == "turn_logits":
                    dve.wait_ge(sd_ready, use + 1)
                    if c >= 1:
                        dve.wait_ge(cb_ready, c)
                    dve.tensor_copy(lt[:, :, :], bank[:, 0:64].rearrange("p (r n) -> p r n", r=4)[:, :, 0:NR]).then_inc(sd_read, 1)
                    dve.wait_ge(sd_read, use + 1)
                    small(dve.tensor_reduce(rs4["mx"][:, :], lt[:, :, 0:NEXP], AX.X, ALU.max))
                    dve.tensor_tensor(rt["d"][:, :, :], lt[:, :, 0:NEXP], rs4["mx"][:, :].unsqueeze(2).broadcast_to([P, 4, NEXP]),
                                      ALU.subtract).then_inc(lt_done, 1)
                elif w == "largest":
                    dve.wait_ge(rt_exp, c + 1)
                    small(dve.tensor_reduce(rs4["sum"][:, :], rt["e"][:, :, :], AX.X, ALU.add))
                    small(dve.reciprocal(rs4["rec"][:, :], rs4["sum"][:, :]))
                    small(dve.tensor_tensor(rt["p"][:, :, :], rt["e"][:, :, :], wide(rs4["rec"]), ALU.mult))
                    pick("p", "m1", "k1", "oh1")
                    small(dve.scalar_tensor_tensor(out=rt["p2"][:, :, :], in0=rt["oh1"][:, :, :], scalar=-4.0,
                                                   in1=rt["p"][:, :, :], op0=ALU.mult, op1=ALU.add))
                elif w == "second":
                    pick("p2", "m2", "k2", "oh2")
                    small(dve.tensor_tensor(rt["oh"][:, :, :], rt["oh1"][:, :, :], rt["oh2"][:, :, :], ALU.add))
                elif w == "combine":
                    small(dve.scalar_tensor_tensor(out=cw[:, :, 0:NEXP], in0=rt["oh"][:, :, :], scalar=0.5, in1=rt["p"][:, :, :],
                                                   op0=ALU.mult, op1=ALU.mult))
                    small(dve.tensor_scalar(cw[:, :, NEXP], sg[:, :], 0.25, 0.25, ALU.mult, ALU.add))
                    if c >= 1:
                        dve.wait_ge(sd_ready, side_use["turn_comb", c - 1] + 1)
                    dve.wait_ge(cb_zero, 1)
                    small(dve.tensor_copy(cbt[:, :, 0:NR], cw[:, :, :]))
                    small(dve.tensor_tensor(cwr[:, 0, :, :], cw[:, :, :], cbt[:, :, 0:NR], ALU.subtract))
                    small(dve.tensor_copy(cbt[:, :, NR:2 * NR], cwr[:, 0, :, :]))
                    small(dve.tensor_tensor(cwr[:, 1, :, :], cwr[:, 0, :, :], cbt[:, :, NR:2 * NR], ALU.subtract))
                    dve.tensor_copy(cbt[:, :, 2 * NR:3 * NR], cwr[:, 1, :, :]).then_inc(cb_ready, 1)
                elif w in ("out_a", "out_b"):
                    first = tiles_of(c).start + 2 * (w == "out_b")
                    t2 = slice(first, first + 2)
                    dve.wait_ge(sd_ready, use + 1)
                    dve.wait_ge(res_x1, c + 1)
                    dve.tensor_tensor(res[:, t2, :], res[:, t2, :], bank[:, :].rearrange("p (r n) -> p r n", r=2),
                                      ALU.add).then_inc(sd_read, 1)
                    dve.wait_ge(sd_read, use + 1)
                    dve.sem_inc(out_ready, 1)

            def read_banks(s, gap):
                for kind, n in BANK_PLAN[s, gap]:
                    if kind == "piece":
                        take_max(n)
                        if n + 1 in PIECE_END:
                            negate(PIECE_END.index(n + 1))
                    elif kind == "ctx":
                        context(n)
                    elif kind == "side":
                        side_dve(EARLY_BANKED[n], 0)

            read_banks(-1, 0)
            dve.wait_ge(mm_ka, NT)
            dve.wait_ge(v_done, NT)
            dve.wait_ge(sx_out, 16 * NT)
            for i in range(2):
                dve.wait_ge(sa_out[i], 16 * (NT // 2))
                dve.wait_ge(sq_out[i], 32 * (NT // 2))
            dve.memset(alog[:, :, :], 0.0).then_inc(a_sum, 1)
            for s in range(NS + 2):
                read_banks(s, 0)
                read_banks(s, 1)
                for kind, t in a_steps.get(s, []):
                    if kind != EXPS:
                        over_heads(kind, t)
                read_banks(s, 2)
                if EARLY.get(s) in ("normalise", "largest", "second", "combine"):
                    side_dve(EARLY[s], 0)
                if s == EARLY_AT - 1:
                    dve.wait_ge(ws_hi, 2)
                    dve.tensor_tensor(wol[:, :, :], woraw[:, :, :], woh[:, :, :].bitcast(F32), ALU.subtract)
                    dve.tensor_tensor(wrl[:, :, :], wrraw[:, :, :], wrh[:, :, :].bitcast(F32), ALU.subtract).then_inc(ws_lo, 1)
                    dve.wait_ge(av_done, STACKS_FREE)
                    dve.memset(cbt[:, :, :], 0.0).then_inc(cb_zero, 1)

            dve.wait_ge(ctx_ready, NU)
            dve.sem_inc(att_end, 1)
            dve.wait_ge(att_end, 4)
            dve.memset(combt[:, :, :], 0.0).then_inc(comb_zero, 1)

            run_side(-1, side_dve)
            for n in range(M3 + 4):
                if n < M3:
                    dve.wait_ge(th_ready, n + 1)
                    if n >= 2:
                        dve.wait_ge(al_ready, n - 1)
                    dve.scalar_tensor_tensor(out=act_f[:, n % 2, :], in0=th[:, n % 2, :], scalar=1.0, in1=pg[n % 2][:, :],
                                             op0=ALU.add, op1=ALU.mult).then_inc(act_step, 1)
                    dve.wait_ge(act_step, 3 * n + 1)
                    dve.wait_ge(u_ready, n + 1)
                    dve.tensor_tensor(act_f[:, n % 2, :], act_f[:, n % 2, :], pu[n % 2][:, :], ALU.mult).then_inc(act_step, 1)
                    dve.wait_ge(act_step, 3 * n + 2)
                    dve.wait_ge(c_ready, n + 1)
                    dve.tensor_tensor(act_f[:, n % 2, :], act_f[:, n % 2, :], pc[:, :], ALU.mult).then_inc(act_step, 1)
                run_side(n, side_dve)
                if n < M3:
                    dve.wait_ge(ah_ready, n + 1)
                    dve.tensor_tensor(act_l[:, n % 2, :], act_f[:, n % 2, :], act_h[:, n % 2, :].bitcast(F32),
                                      ALU.subtract).then_inc(al_ready, 1)

        @block.tensor
        def _(pe):
            def three(dst, a_hi, a_lo, b_hi, b_lo, k):
                pe.matmul(dst, a_hi, b_hi, start=(k == 0), stop=False)
                pe.matmul(dst, a_hi, b_lo, start=False, stop=False)
                return pe.matmul(dst, a_lo, b_hi, start=False, stop=(k == KC - 1))

            def turn_x(t, par):
                pe.wait_ge(xn_done, t + 1)
                if at_least(t, 1):
                    pe.wait_ge(x_lo, t)
                for k in range(KC):
                    last = pe.transpose(tp[:, k * P:(k + 1) * P], xnp[:, par, k * P:(k + 1) * P], ident)
                last.then_inc(tp_ready, 1)

            def turn_q(t, par):
                pe.wait_ge(roped, t + 1)
                if at_least(t, 1):
                    pe.wait_ge(q_lo, t)
                for f in range(4):
                    last = pe.transpose(qt[:, f, :], qkr[:, par, f * P:(f + 1) * P], ident)
                last.then_inc(qt_ready, 1)

            pe.wait_ge(id_in, 16)
            turn_x(0, 0)

            def step(m, par):
                t = 2 * m + par
                if at_most(t, NT - 2):
                    turn_x(t + 1, 1 - par)
                pe.wait_ge(x_lo, t + 1)
                if at_least(t, 2):
                    pe.wait_ge(e_a, t - 1)
                for n, (dst, done) in enumerate(((pqk, mm_qk), (pva, mm_va), (pka, mm_ka))):
                    if isinstance(t, int) and t == 0:
                        pe.wait_ge(w_lo, n + 1)
                    w = slice(n * CH, (n + 1) * CH)
                    for k in range(KC):
                        last = three(dst[par][:, :], xh[:, par, k, :], xl[:, par, k, :], wh[:, k, w], wl[:, k, w], k)
                    last.then_inc(done, 1)
                if at_least(t, 1):
                    turn_q(t - 1, 1 - par)

            tiles(pe, step)
            turn_q(NT - 1, 1)
            pe.wait_ge(q_lo, NT)
            pe.wait_ge(e_a, NT)
            pe.wait_ge(cst_bf, 1)
            pe.wait_ge(v_ones, 1)
            pe.wait_ge(v_done, NT)

            def max_piece(i, bank):
                u, r, pairs, e, k0, w, diagonal = PIECES[i]
                g, c = UNITS[u]
                if i == 0:
                    pe.wait_ge(stk_first, 16 * 12)
                if i == PIECE_END[FIRST_COLS // CH - 1] or i > 0 and UNITS[PIECES[i - 1][0]][0] != g:
                    pe.wait_ge(stk_in[g % 2], 16 * 12 if g < 2 else 16 * 25)
                q0 = c * CH + r * P
                for n, pair in enumerate(pairs):
                    last = pe.matmul(bank[:, n * w:(n + 1) * w], qs[g % 2][:, pair, e, q0:q0 + P],
                                     ks[g % 2][:, pair, k0:k0 + w], start=True, stop=not diagonal)
                    if diagonal:
                        last = pe.matmul(bank[:, (n + 1) * w - P:(n + 1) * w], identb[:, :], mmaxb[:, :],
                                         start=False, stop=True)
                last.then_inc(mx_ready, 1)

            def side_pe(w, c):
                if w not in BANKED:
                    return
                use = side_use[w, c]
                bank = side_bank(w, c)
                if use:
                    pe.wait_ge(sd_read, use)
                if w in ("turn_ctx0", "turn_ctx1", "turn_h0", "turn_h1"):
                    k = int(w[-1])
                    if w.startswith("turn_ctx"):
                        pe.wait_ge(cx_in, 16 * (c + 1))
                    else:
                        pe.wait_ge(hn_ready, c + 1)
                    for r in range(4):
                        last = pe.transpose(bank[:, r * P:(r + 1) * P], ctxin[:, r, k * P:(k + 1) * P], ident)
                elif w in ("proj_a", "proj_b"):
                    pe.wait_ge(ws_lo, 1)
                    for r in range(2):
                        tok = slice((2 * (w == "proj_b") + r) * P, (2 * (w == "proj_b") + r + 1) * P)
                        for k in range(KC):
                            last = three(bank[:, r * D:(r + 1) * D], cth[:, k, tok], ctl[:, k, tok], woh[:, k, :], wol[:, k, :], k)
                elif w == "logits":
                    for k in range(KC):
                        last = three(bank[0:NR, :], wrh[:, k, :], wrl[:, k, :], hth[:, c % 2, k, :], htl[:, c % 2, k, :], k)
                elif w == "turn_logits":
                    for r in range(4):
                        last = pe.transpose(bank[:, 16 * r:16 * r + NR], lg[:, r * P:(r + 1) * P], cst[0:NR, C_ID:C_ID + NR])
                elif w == "turn_comb":
                    pe.wait_ge(cb_ready, c + 1)
                    for r in range(4):
                        last = pe.transpose(bank[:, :].bitcast(BF16)[0:32, r * P:(r + 1) * P], cbt[:, r, :], identb[:, :])
                else:
                    pe.wait_ge(y_read, c + 1)
                    for i in range(2):
                        r = 2 * (w == "out_b") + i
                        for f in range(2):
                            y = x1[:, 2 * f:2 * f + 2, :].rearrange("p a n -> p (a n)")
                            last = pe.transpose(bank[:, i * D + f * P:i * D + (f + 1) * P], y[:, r * P:(r + 1) * P], ident)
                last.then_inc(sd_ready, 1)

            def bank_use(kind, n):
                at = BANK_AT[kind, n]
                bank = mx[at % 3]
                if at >= 3:
                    k, i = BANK_USES[at - 3]
                    pe.wait_ge({"piece": mx_read, "neg": nr_ready, "ctx": ctx_ready, "side": sd_read}[k], i + 1)
                if kind == "piece":
                    max_piece(n, bank)
                elif kind == "neg":
                    pe.wait_ge(nm_ready, n + 1)
                    for r in range(CH // P):
                        last = pe.transpose(bank[0:8, r * P:(r + 1) * P], nmt[:, n % 2, r, :].bitcast(F32), ident)
                    last.then_inc(nt_ready, 1)
                elif kind == "side":
                    side_pe(EARLY_BANKED[n], 0)
                else:
                    pe.wait_ge(o_read, n + 1)
                    for r in range(CH // P):
                        last = pe.transpose(bank[:, r * P:(r + 1) * P], osb[:, r * P:(r + 1) * P], ident)
                    last.then_inc(ot_ready, 1)

            def bank_uses(s, gap):
                for use in BANK_PLAN[s, gap]:
                    bank_use(*use)

            def scores(s, pr):
                u, kb = STEPS[s]
                g, c = UNITS[u]
                off = first_key_column(s)
                if s >= 1:
                    pe.wait_ge(exped, 2 * s + pr - 1)
                for e in range(2):
                    diagonal = kb * P >= c * CH
                    last = pe.matmul(st[pr][:, e, off:CH], ks[g % 2][:, pr, kb * P:(kb + 1) * P],
                                     qs[g % 2][:, pr, e, c * CH + off:(c + 1) * CH], start=True, stop=not diagonal)
                    if diagonal:
                        last = pe.matmul(st[pr][:, e, off:off + P], identb[:, :], mstb[:, :], start=False, stop=True)
                last.then_inc(st_ready, 1)

            def weigh(s):
                u, kb = STEPS[s]
                g, c = UNITS[u]
                off = first_key_column(s)
                pe.wait_ge(exped, 2 * s + 2)
                if kb == 0 and u >= 1:
                    pe.wait_ge(o_read, u)
                for j in range(G):
                    last = pe.matmul(o[32 * j:32 * j + VC, off:CH], v[:, kb, 4 * g + j, :],
                                     pt[:, s % 2, j // 2, j % 2, off:CH], start=(kb == 0), stop=(kb == 4 * c + 3))
                last.then_inc(av_done, 1)

            def before_scores(s):
                u, kb = STEPS[s]
                if kb == 0:
                    pe.wait_ge(nr_in[u % 4], 32 * (u // 4 + 1))

            pe.matmul(o[:, :], zb[:, 0:P], zb[:, :], start=True, stop=True).then_inc(o_zero, 1)
            bank_uses(-1, 0)
            before_scores(0)
            scores(0, 0)
            scores(0, 1)
            for s in range(NS + 2):
                if s < NS - 1:
                    before_scores(s + 1)
                    scores(s + 1, 0)
                bank_uses(s, 0)
                if s < NS - 1:
                    scores(s + 1, 1)
                bank_uses(s, 1)
                if s < NS:
                    weigh(s)
                bank_uses(s, 2)

            pe.wait_ge(ctx_ready, NU)
            pe.sem_inc(att_end, 1)
            pe.wait_ge(att_end, 4)

            def down(n):
                c, ic = divmod(n, NIC)
                pe.wait_ge(al_ready, n + 1)
                if ic == 0 and c >= 1:
                    pe.wait_ge(y_read, c)
                for f in range(2):
                    for i, (a, b) in enumerate(((mh, act_h), (mh, act_l), (ml, act_h))):
                        last = pe.matmul(py[f][:, :], a[ic][:, 4 + f, :], b[:, n % 2, :],
                                         start=(ic == 0 and i == 0), stop=(ic == NIC - 1 and i == 2))
                last.then_inc(y_used, 1)

            run_side(-1, side_pe)
            for n in range(M3 + 4):
                c, ic = divmod(n, NIC)
                if 2 <= n < M3 + 2:
                    down(n - 2)
                if n < M3:
                    if c == 0:
                        pe.wait_ge(m_lo, ic + 1)
                    if n >= 2:
                        pe.wait_ge(act_step, 3 * (n - 2) + 2)
                    for dst, at, done in ((pg, 0, g_ready), (pu, 2, u_ready)):
                        for k in range(KC):
                            last = three(dst[n % 2][:, :], mh[ic][:, at + k, :], ml[ic][:, at + k, :],
                                         hth[:, c % 2, k, :], htl[:, c % 2, k, :], k)
                        last.then_inc(done, 1)
                    if ic == 0:
                        pe.wait_ge(sd_read, side_use["turn_comb", c] + 1)
                    if n == 0:
                        pe.wait_ge(sel_in, 16)
                        pe.wait_ge(comb_zero, 1)
                    if n >= 1:
                        pe.wait_ge(act_step, 3 * (n - 1) + 3)
                    pe.matmul(pc[:, :], selb[:, ic * P:(ic + 1) * P], combt[:, c % 2, :], start=True, stop=True).then_inc(c_ready, 1)
                run_side(n, side_pe)


def kernel(**inputs):
    import numpy as np
    import concourse.bacc as bacc
    from concourse.bass_utils import run_bass_kernel_spmd

    a = {n: np.asarray(v) for n, v in inputs.items()}
    f = {n[len("L0_ffn_"):]: v for n, v in a.items() if n.startswith("L0_ffn_")}
    wide = lambda w: w.transpose(1, 0, 2).reshape(D, -1)
    pad = NIC * P - I_ALL
    gate = np.pad(np.concatenate([wide(f["w_gate_e"]), f["w_sh_gate"]], 1), ((0, 0), (0, pad)))
    up = np.pad(np.concatenate([wide(f["w_up_e"]), f["w_sh_up"]], 1), ((0, 0), (0, pad)))
    down = np.pad(np.concatenate([f["w_down_e"].reshape(-1, D), f["w_sh_down"]], 0), ((0, pad), (0, 0)))
    split = lambda w: w.reshape(KC, P, NIC, P).transpose(2, 1, 0, 3).reshape(NIC, P, KC * P)
    arrays = {
        "x": a["L0_attn_input_seq_embs"][0],
        "wproj": np.concatenate([f["wq"], f["wk"], f["wv"]] + [a[f"L0_attn_W{n}"].T for n in "qkv"], 1),
        "bqkv": np.concatenate([f["bq"], f["bk"], f["bv"]]),
        "wln": np.stack([f["w_ln1"], f["w_ln2"]]).reshape(2, KC, P).transpose(2, 0, 1),
        "wo": f["wo"],
        "wr": np.concatenate([f["w_router"], f["w_sh_eg"]], 1),
        "wmoe": np.concatenate([split(gate), split(up), down.reshape(NIC, P, D)], 2),
    }
    pos = np.arange(T, dtype=np.float32).reshape(NT, P).T
    inv = (1.0 / THETA ** (np.arange(0, HD, 2, dtype=np.float32) / HD)).astype(np.float32)
    ang = pos[:, :, None] * inv
    cos, sin = np.cos(ang), np.sin(ang)
    row, col = np.arange(P)[:, None], np.arange(P)[None, :]
    heads = np.where(np.arange(H)[None, :] > np.arange(H)[:, None], NEG, 0.0).reshape(1, -1)
    scale = HD ** -0.5
    consts = np.concatenate([
        np.eye(P), np.where(col > row, NEG, 0.0), np.where(col < row, NEG, 0.0), np.repeat(heads, P, 0),
        np.stack([cos * scale, cos], 2).reshape(P, -1),
        np.stack([np.stack([-sin, sin], 2) * scale, np.stack([-sin, sin], 2)], 2).reshape(P, -1),
        np.repeat(np.arange(NEXP, 0, -1)[None, :], P, 0),
    ], 1).astype(np.float32)
    owner = np.minimum(np.arange(NIC * P) // MOE_I, NEXP)
    sel = np.tile((owner[None, :] == np.arange(NR)[:, None]).astype(np.float32), (3, 1))
    arrays["consts"], arrays["sel"] = consts, sel

    nc = bacc.Bacc("TRN2", target_bir_lowering=False, num_devices=1)
    arrays = {n: np.ascontiguousarray(v) for n, v in arrays.items()}
    io = {n: nc.dram_tensor(n, v.shape, mybir.dt.from_np(v.dtype), kind="ExternalInput").ap() for n, v in arrays.items()}
    io["out"] = nc.dram_tensor("out", (T, D), F32, kind="ExternalOutput").ap()
    for name, shape in (("sq", (2, 2 * D, T)), ("sa", (NT, P, 3 * D)), ("sx", (P, NT, D)), ("sn", (NU, 8, CH)), ("sc", (P, NT, D)), ("sz", (2, 2, 2, T))):
        io[name] = nc.dram_tensor(name, shape, F32, kind="Internal").ap()
    block_program(nc, **io)
    r = run_bass_kernel_spmd(nc, [arrays], core_ids=[0])
    return r.results[0]["out"].reshape(1, T, D)
```
